# Optimizing a Trainium2 kernel written in Bass

```python
import numpy as np
import jax
import jax.numpy as jnp

def _softmax(x, axis=-1):
    return jax.nn.softmax(x, axis=axis)

def _gelu(x):
    return jax.nn.gelu(x, approximate=True)

def _silu(x):
    return jax.nn.silu(x)

def _sigmoid(x):
    return jax.nn.sigmoid(x)

def _layernorm(x, axis=-1, eps=1e-05):
    m = jnp.mean(x, axis=axis, keepdims=True)
    v = jnp.var(x, axis=axis, keepdims=True)
    return (x - m) / jnp.sqrt(v + eps)

def _scatter_add(tgt, idx, src, axis=0):
    return tgt.at[idx].add(src)

def _segment_sum(src, seg, n):
    return jax.ops.segment_sum(src, seg, n)
kernel_name = 'mk_xattn_ffn_d2_seqx_r2_665be1'

def setup_inputs(seed: int=0):
    np.random.seed(seed)
    _w = jnp.asarray

    def _rec_inputs():
        import jax
        import jax.numpy as jnp
        _rk = jax.random.key(seed)
        x = -0.0002928 + 1 * jax.random.normal(jax.random.fold_in(_rk, 1), (8, 100, 1024), jnp.float32)
        _lenS = 100 - jax.random.randint(jax.random.fold_in(_rk, 7), (8,), 0, max(1, 100 // 4) + 1, jnp.int32)
        _lenS2 = 722 - jax.random.randint(jax.random.fold_in(_rk, 8), (8,), 0, max(1, 722 // 4) + 1, jnp.int32)
        _ctx_512P = jax.random.normal(jax.random.fold_in(_rk, 11), (8, 16, 256), jnp.float32)
        _ctx_512c = jax.random.dirichlet(jax.random.fold_in(_rk, 511), 0.3 * jnp.ones((16,), jnp.float32), (8, 722))
        _ctx_512t = jnp.einsum('bsk,bkd->bsd', _ctx_512c, _ctx_512P)
        _ctx_512t = _ctx_512t * jax.lax.rsqrt(jnp.mean(jnp.square(_ctx_512t)) + 1e-12) * 0.953939
        ctx_512 = 0.000227908 + 0.99994 * (_ctx_512t + 0.3 * jax.random.normal(jax.random.fold_in(_rk, 611), (8, 722, 256), jnp.float32))
        return (x, ctx_512)
    x, ctx_512 = _rec_inputs()

    def _L0_xattn_setup():
        import jax, jax.numpy as jnp
        import numpy as np
        B, S, L = (2, 512, 512)
        DIM_Q, H, K, D_C, D_CQ, R = (1024, 16, 128, 256, 768, 64)

        def _rope_tables(length, dim):
            inv = 1.0 / 10000.0 ** (jnp.arange(0, dim, 2, dtype=jnp.float32) / dim)
            f = jnp.arange(length, dtype=jnp.float32)[:, None] * inv[None, :]
            sin = jnp.repeat(jnp.sin(f), 2, axis=-1)
            cos = jnp.repeat(jnp.cos(f), 2, axis=-1)
            return (sin, cos)

        def _rotate_half(x):
            half = x.shape[-1] // 2
            return jnp.concatenate([-x[..., half:], x[..., :half]], axis=-1)

        def _apply_rope(x, sin, cos):
            return x * cos + _rotate_half(x) * sin
        key = jax.random.key(seed)
        ks = jax.random.split(key, 8)
        return {'hidden_q': jax.random.normal(ks[0], (B, S, DIM_Q), jnp.float32), 'kv_c': jax.random.normal(ks[1], (B, L, D_C), jnp.float32), 'Wq': jax.random.normal(ks[2], (H * K, DIM_Q), jnp.float32) / np.sqrt(DIM_Q).astype(np.float32), 'w_kc_q': jax.random.normal(ks[3], (H, K, D_CQ), jnp.float32) / np.sqrt(K).astype(np.float32), 'w_kc_kv': jax.random.normal(ks[4], (H, K, D_C), jnp.float32) / np.sqrt(K).astype(np.float32), 'W_qr': jax.random.normal(ks[5], (H, D_CQ, R), jnp.float32) / np.float32(np.sqrt(D_CQ) * np.sqrt(R)), 'W_kr': jax.random.normal(ks[6], (H, D_C, R), jnp.float32) / np.sqrt(D_C).astype(np.float32), 'Wo': jax.random.normal(ks[7], (DIM_Q, H * K), jnp.float32) / np.sqrt(H * K).astype(np.float32)}
    _L0_xattn_all = _L0_xattn_setup()
    _L0_xattn_in = {k: v for k, v in _L0_xattn_all.items() if k in ('Wq', 'w_kc_q', 'w_kc_kv', 'W_qr', 'W_kr', 'Wo')}
    del _L0_xattn_all

    def _L0_ffn_setup():
        import jax, jax.numpy as jnp
        import numpy as np
        SWIGLU_ALPHA = 1.702
        SWIGLU_LIMIT = 7.0
        B, S, H, E, K, I = (2, 1024, 1024, 32, 4, 512)
        key = jax.random.key(seed)
        ks = jax.random.split(key, 8)
        return {'hidden_states': jax.random.normal(ks[0], (B, S, H), jnp.float32), 'gate_w': jax.random.normal(ks[1], (E, H), jnp.float32) * 0.02, 'gate_b': jnp.zeros((E,), jnp.float32), 'w_gate': jax.random.normal(ks[2], (E, H, I), jnp.float32) * 0.02, 'b_gate': jnp.zeros((E, I), jnp.float32), 'w_up': jax.random.normal(ks[3], (E, H, I), jnp.float32) * 0.02, 'b_up': jnp.zeros((E, I), jnp.float32), 'w_down': jax.random.normal(ks[4], (E, I, H), jnp.float32) * 0.02, 'b_down': jnp.zeros((E, H), jnp.float32)}
    _L0_ffn_all = _L0_ffn_setup()
    _L0_ffn_in = {k: v for k, v in _L0_ffn_all.items() if k in ('gate_w', 'gate_b', 'w_gate', 'b_gate', 'w_up', 'b_up', 'w_down', 'b_down')}
    del _L0_ffn_all

    def _L1_xattn_setup():
        import jax, jax.numpy as jnp
        import numpy as np
        B, S, L = (2, 512, 512)
        DIM_Q, H, K, D_C, D_CQ, R = (1024, 16, 128, 256, 768, 64)

        def _rope_tables(seq_len, dim, dtype):
            inv_freq = 1.0 / 10000.0 ** (jnp.arange(0, dim, 2, dtype=dtype) / dim)
            t = jnp.arange(seq_len, dtype=dtype)
            freqs = t[:, None] * inv_freq[None, :]
            sin = jnp.repeat(jnp.sin(freqs), 2, axis=-1)
            cos = jnp.repeat(jnp.cos(freqs), 2, axis=-1)
            return (sin, cos)

        def _rotate_half(x):
            h = x.shape[-1] // 2
            return jnp.concatenate([-x[..., h:], x[..., :h]], axis=-1)
        key = jax.random.key(seed)
        ks = jax.random.split(key, 8)
        s_in = 1.0 / np.sqrt(DIM_Q)
        s_k = 1.0 / np.sqrt(K)
        s_cq = 1.0 / np.sqrt(D_CQ)
        s_c = 1.0 / np.sqrt(D_C)
        return {'hidden_q': jax.random.normal(ks[0], (B, S, DIM_Q), jnp.float32), 'kv_c': jax.random.normal(ks[1], (B, L, D_C), jnp.float32), 'Wq': jax.random.normal(ks[2], (H * K, DIM_Q), jnp.float32) * s_in, 'w_kc_q': jax.random.normal(ks[3], (H, K, D_CQ), jnp.float32) * s_k, 'w_kc_kv': jax.random.normal(ks[4], (H, K, D_C), jnp.float32) * s_k, 'W_qr': jax.random.normal(ks[5], (H, D_CQ, R), jnp.float32) * s_cq / np.sqrt(R), 'W_kr': jax.random.normal(ks[6], (H, D_C, R), jnp.float32) * s_c, 'Wo': jax.random.normal(ks[7], (DIM_Q, H * K), jnp.float32) * s_k}
    _L1_xattn_all = _L1_xattn_setup()
    _L1_xattn_in = {k: v for k, v in _L1_xattn_all.items() if k in ('Wq', 'w_kc_q', 'w_kc_kv', 'W_qr', 'W_kr', 'Wo')}
    del _L1_xattn_all

    def _L1_ffn_setup():
        import jax, jax.numpy as jnp
        import numpy as np
        D_MODEL = 1024
        D_EXPERT = 4096
        EPS = 1e-08

        def ternary_quant(w):
            scale = jnp.mean(jnp.abs(w)) + EPS
            q = jnp.clip(jnp.round(w / scale), -1.0, 1.0) * scale
            return w + jax.lax.stop_gradient(q - w)
        key = jax.random.key(seed)
        k_x, k_up, k_gate, k_down = jax.random.split(key, 4)
        std_in = 1.0 / np.sqrt(D_MODEL)
        std_exp = 1.0 / np.sqrt(D_EXPERT)
        return {'x': jax.random.normal(k_x, (4, 1024, D_MODEL), dtype=jnp.float32), 'W_up': jax.random.normal(k_up, (D_EXPERT, D_MODEL), dtype=jnp.float32) * std_in, 'W_gate': jax.random.normal(k_gate, (D_EXPERT, D_MODEL), dtype=jnp.float32) * std_in, 'W_down': jax.random.normal(k_down, (D_MODEL, D_EXPERT), dtype=jnp.float32) * std_exp}
    _L1_ffn_all = _L1_ffn_setup()
    _L1_ffn_in = {k: v for k, v in _L1_ffn_all.items() if k in ('W_up', 'W_gate', 'W_down')}
    del _L1_ffn_all
    return {'x': x, 'ctx_512': ctx_512, 'L0_xattn_Wq': _L0_xattn_in['Wq'], 'L0_xattn_w_kc_q': _L0_xattn_in['w_kc_q'], 'L0_xattn_w_kc_kv': _L0_xattn_in['w_kc_kv'], 'L0_xattn_W_qr': _L0_xattn_in['W_qr'], 'L0_xattn_W_kr': _L0_xattn_in['W_kr'], 'L0_xattn_Wo': _L0_xattn_in['Wo'], 'L0_ffn_gate_w': _L0_ffn_in['gate_w'], 'L0_ffn_gate_b': _L0_ffn_in['gate_b'], 'L0_ffn_w_gate': _L0_ffn_in['w_gate'], 'L0_ffn_b_gate': _L0_ffn_in['b_gate'], 'L0_ffn_w_up': _L0_ffn_in['w_up'], 'L0_ffn_b_up': _L0_ffn_in['b_up'], 'L0_ffn_w_down': _L0_ffn_in['w_down'], 'L0_ffn_b_down': _L0_ffn_in['b_down'], 'L1_xattn_Wq': _L1_xattn_in['Wq'], 'L1_xattn_w_kc_q': _L1_xattn_in['w_kc_q'], 'L1_xattn_w_kc_kv': _L1_xattn_in['w_kc_kv'], 'L1_xattn_W_qr': _L1_xattn_in['W_qr'], 'L1_xattn_W_kr': _L1_xattn_in['W_kr'], 'L1_xattn_Wo': _L1_xattn_in['Wo'], 'L1_ffn_W_up': _L1_ffn_in['W_up'], 'L1_ffn_W_gate': _L1_ffn_in['W_gate'], 'L1_ffn_W_down': _L1_ffn_in['W_down']}

def reference(x, ctx_512, L0_xattn_Wq, L0_xattn_w_kc_q, L0_xattn_w_kc_kv, L0_xattn_W_qr, L0_xattn_W_kr, L0_xattn_Wo, L0_ffn_gate_w, L0_ffn_gate_b, L0_ffn_w_gate, L0_ffn_b_gate, L0_ffn_w_up, L0_ffn_b_up, L0_ffn_w_down, L0_ffn_b_down, L1_xattn_Wq, L1_xattn_w_kc_q, L1_xattn_w_kc_kv, L1_xattn_W_qr, L1_xattn_W_kr, L1_xattn_Wo, L1_ffn_W_up, L1_ffn_W_gate, L1_ffn_W_down):
    import jax
    import jax.numpy as jnp

    def _L0_xattn_ref(hidden_q, kv_c, Wq, w_kc_q, w_kc_kv, W_qr, W_kr, Wo):
        import jax, jax.numpy as jnp
        import numpy as np
        B, S, L = (2, 512, 512)
        DIM_Q, H, K, D_C, D_CQ, R = (1024, 16, 128, 256, 768, 64)

        def _rope_tables(length, dim):
            inv = 1.0 / 10000.0 ** (jnp.arange(0, dim, 2, dtype=jnp.float32) / dim)
            f = jnp.arange(length, dtype=jnp.float32)[:, None] * inv[None, :]
            sin = jnp.repeat(jnp.sin(f), 2, axis=-1)
            cos = jnp.repeat(jnp.cos(f), 2, axis=-1)
            return (sin, cos)

        def _rotate_half(x):
            half = x.shape[-1] // 2
            return jnp.concatenate([-x[..., half:], x[..., :half]], axis=-1)

        def _apply_rope(x, sin, cos):
            return x * cos + _rotate_half(x) * sin
        Bv, Sv, _ = hidden_q.shape
        _, Lv, _ = kv_c.shape
        q_hk = (hidden_q @ Wq.T).reshape(Bv, Sv, H, K)
        q_big = jnp.einsum('bshk,hkq->bshq', q_hk, w_kc_q)
        sin_q, cos_q = _rope_tables(Sv, D_CQ)
        q_big = _apply_rope(q_big, sin_q[None, :, None, :], cos_q[None, :, None, :])
        sin_k, cos_k = _rope_tables(Lv, D_C)
        kv_r = _apply_rope(kv_c, sin_k[None], cos_k[None])
        q_r = jnp.einsum('bshq,hqr->bhsr', q_big, W_qr)
        k_r = jnp.einsum('bld,hdr->bhlr', kv_r, W_kr)
        scores = jnp.einsum('bhsr,bhlr->bhsl', q_r, k_r)
        attn = jax.nn.softmax(scores, axis=-1)
        ctx_c = jnp.einsum('bhsl,bld->bhsd', attn, kv_r)
        ctx_lat = jnp.einsum('bhsd,hkd->bhsk', ctx_c, w_kc_kv)
        ctx = ctx_lat.transpose(0, 2, 1, 3).reshape(Bv, Sv, H * K)
        return ctx @ Wo.T

    def _L0_ffn_ref(hidden_states, gate_w, gate_b, w_gate, b_gate, w_up, b_up, w_down, b_down):
        import jax, jax.numpy as jnp
        import numpy as np
        SWIGLU_ALPHA = 1.702
        SWIGLU_LIMIT = 7.0
        B, S, H, E, K, I = (2, 1024, 1024, 32, 4, 512)
        Bb, Ss, Hh = hidden_states.shape
        x = hidden_states.reshape(-1, Hh)
        logits = x @ gate_w.T + gate_b
        topk_logits, topk_idx = jax.lax.top_k(logits, K)
        topk_weight = jax.nn.softmax(topk_logits.astype(jnp.float32), axis=-1)
        flat_idx = topk_idx.reshape(-1)
        xs = jnp.repeat(x, K, axis=0)
        order = jnp.argsort(flat_idx)
        xt = xs[order]
        gid = flat_idx[order]
        group_sizes = jnp.bincount(flat_idx, length=E).astype(jnp.int32)
        gate = jax.lax.ragged_dot(xt, w_gate, group_sizes) + b_gate[gid]
        up = jax.lax.ragged_dot(xt, w_up, group_sizes) + b_up[gid]
        gate = jnp.minimum(gate, SWIGLU_LIMIT)
        up = jnp.clip(up, -SWIGLU_LIMIT, SWIGLU_LIMIT)
        glu = gate * jax.nn.sigmoid(SWIGLU_ALPHA * gate)
        activated = (up + 1.0) * glu
        outs = jax.lax.ragged_dot(activated, w_down, group_sizes) + b_down[gid]
        inv = jnp.argsort(order)
        outs = outs[inv].reshape(-1, K, Hh)
        y = jnp.sum(outs * topk_weight[..., None], axis=1).astype(x.dtype)
        return y.reshape(Bb, Ss, Hh)

    def _L1_xattn_ref(hidden_q, kv_c, Wq, w_kc_q, w_kc_kv, W_qr, W_kr, Wo):
        import jax, jax.numpy as jnp
        import numpy as np
        B, S, L = (2, 512, 512)
        DIM_Q, H, K, D_C, D_CQ, R = (1024, 16, 128, 256, 768, 64)

        def _rope_tables(seq_len, dim, dtype):
            inv_freq = 1.0 / 10000.0 ** (jnp.arange(0, dim, 2, dtype=dtype) / dim)
            t = jnp.arange(seq_len, dtype=dtype)
            freqs = t[:, None] * inv_freq[None, :]
            sin = jnp.repeat(jnp.sin(freqs), 2, axis=-1)
            cos = jnp.repeat(jnp.cos(freqs), 2, axis=-1)
            return (sin, cos)

        def _rotate_half(x):
            h = x.shape[-1] // 2
            return jnp.concatenate([-x[..., h:], x[..., :h]], axis=-1)
        b, s, _ = hidden_q.shape
        l = kv_c.shape[1]
        q_hk = (hidden_q @ Wq.T).reshape(b, s, H, K)
        q_big = jnp.einsum('bshk,hkq->bshq', q_hk, w_kc_q)
        sin, cos = _rope_tables(l, D_C, kv_c.dtype)
        kv_rope = kv_c * cos[None] + _rotate_half(kv_c) * sin[None]
        q_r = jnp.einsum('bshq,hqr->bhsr', q_big, W_qr)
        k_r = jnp.einsum('bld,hdr->bhlr', kv_rope, W_kr)
        scores = jnp.einsum('bhsr,bhlr->bhsl', q_r, k_r)
        attn = jax.nn.softmax(scores, axis=-1)
        ctx_c = jnp.einsum('bhsl,bld->bhsd', attn, kv_rope)
        ctx_lat = jnp.einsum('bhsd,hkd->bshk', ctx_c, w_kc_kv)
        out = ctx_lat.reshape(b, s, H * K) @ Wo.T
        return out

    def _L1_ffn_ref(x, W_up, W_gate, W_down):
        import jax, jax.numpy as jnp
        import numpy as np
        D_MODEL = 1024
        D_EXPERT = 4096
        EPS = 1e-08

        def ternary_quant(w):
            scale = jnp.mean(jnp.abs(w)) + EPS
            q = jnp.clip(jnp.round(w / scale), -1.0, 1.0) * scale
            return w + jax.lax.stop_gradient(q - w)
        wu = ternary_quant(W_up)
        wg = ternary_quant(W_gate)
        wd = ternary_quant(W_down)
        up = jnp.einsum('bsd,ed->bse', x, wu)
        gate = jnp.einsum('bsd,ed->bse', x, wg)
        hidden = jax.nn.silu(up) * gate
        return jnp.einsum('bse,de->bsd', hidden, wd)
    x = x + _L0_xattn_ref(_layernorm(x, axis=-1), ctx_512, L0_xattn_Wq, L0_xattn_w_kc_q, L0_xattn_w_kc_kv, L0_xattn_W_qr, L0_xattn_W_kr, L0_xattn_Wo)
    x = x + _L0_ffn_ref(_layernorm(x, axis=-1), L0_ffn_gate_w, L0_ffn_gate_b, L0_ffn_w_gate, L0_ffn_b_gate, L0_ffn_w_up, L0_ffn_b_up, L0_ffn_w_down, L0_ffn_b_down)
    x = x + _L1_xattn_ref(_layernorm(x, axis=-1), ctx_512, L1_xattn_Wq, L1_xattn_w_kc_q, L1_xattn_w_kc_kv, L1_xattn_W_qr, L1_xattn_W_kr, L1_xattn_Wo)
    x = x + _L1_ffn_ref(_layernorm(x, axis=-1), L1_ffn_W_up, L1_ffn_W_gate, L1_ffn_W_down)
    return x

_drawn_inputs = setup_inputs


def setup_inputs(seed=0):
    import zlib

    import numpy as np

    out = dict(_drawn_inputs(seed))
    spreads = {'L0_ffn_gate_b': (0.0, 0.368),
     'L0_ffn_b_gate': (0.0, 0.8),
     'L0_ffn_b_up': (0.0, 0.8),
     'L0_ffn_b_down': (0.0, 0.311)}
    factors = {}
    for name, (base, spread) in spreads.items():
        noise = np.random.default_rng([zlib.crc32(name.encode()), seed]).standard_normal(out[name].shape)
        drawn = base * np.exp(spread * noise) if base else spread * noise
        out[name] = jnp.asarray(drawn.astype(out[name].dtype))
    for name, factor in factors.items():
        out[name] = (out[name] * factor).astype(out[name].dtype)
    return out
```

```python
from contextlib import ExitStack

import numpy as np

import concourse.bass as bass
from concourse import mybir

F32 = mybir.dt.float32
F16 = mybir.dt.float16
I32 = mybir.dt.int32
U32 = mybir.dt.uint32
ALU = mybir.AluOpType
ACT = mybir.ActivationFunctionType
AX = mybir.AxisListType.X

P = 128
B, S, D = 8, 100, 1024
L, DC = 722, 256
H, K, DQ, R = 16, 128, 768, 64
E, TOPK, FI = 32, 4, 512
FE = 4096
T = B * S
MT = -(-T // P)
TW = [min(P, T - P * m) for m in range(MT)]
TPAD = MT * P
KC = D // P
LC = -(-L // P)
LREST = L - (LC - 1) * P
LPAD = LC * P
QC = DQ // P
CC = DC // P
HA = 4
HG = H // HA
BH = 4
HALF = BH * S
GW = HA * S
NQ = 6 * HA
QG = P // E
IC = FI // P
MAX_TILES = (T * TOPK + E * P) // P - 1
MAX_PAIRS = MAX_TILES // 2
RUN = 3
assert (MAX_PAIRS - 1) % RUN == 0
FILL = -(-(2 * MAX_PAIRS - E) // HG)
IDXW = MAX_TILES + 2
EARLY = MT
KPOOL = 1
EC = FE // P
NBLK = 2
EB = EC // NBLK
EPS = 1e-5
TERN_EPS = 1e-8
ALPHA, LIMIT = 1.702, 7.0
XS = 1024.0
HSC = 2.0 ** -5
NEG = -1e30

WQ_N = KC * K
WC_C, WC_R, WC_K = 0, DQ, DQ + QC * R
WC_N = WC_K + 2 * DC
WB_V, WB_O = 0, HA * CC * K
WB_N = WB_O + HA * D
W2_D = KC * 2 * FI
W2_N = W2_D + IC * D

C_ID, C_ONE, C_TRI, C_SLOT = 0, P, 2 * P, 3 * P
C_TILE = 4 * P
C_TIX = C_TILE + MAX_TILES
C_PAD = C_TIX + IDXW
C_TID = C_PAD + 1
C_VAL = C_TID + MT
C_PIX = C_VAL + MT
C_FOLD = C_PIX + 1
C_N = C_FOLD + TW[-1]
assert HA * TW[-1] == P


def constants():
    c = np.zeros((P, C_N), np.float32)
    c[:, C_ID:C_ID + P] = np.eye(P)
    c[:, C_ONE:C_ONE + P] = 1
    c[:, C_TRI:C_TRI + P] = np.triu(np.ones((P, P)), 1)
    c[:, C_SLOT:C_SLOT + P] = np.arange(P)
    c[:, C_TILE:C_TILE + MAX_TILES] = P * np.arange(MAX_TILES)
    c[:, C_TIX:C_TIX + IDXW] = np.arange(IDXW)
    c[LREST:, C_PAD] = NEG
    tok = np.arange(TPAD).reshape(MT, P).T
    c[:, C_TID:C_TID + MT] = np.where(tok < T, tok, 0)
    c[:, C_VAL:C_VAL + MT] = tok < T
    c[:, C_PIX] = np.arange(P)
    c[:, C_FOLD:C_FOLD + TW[-1]] = np.tile(np.eye(TW[-1]), (HA, 1))

    def table(length, dim):
        inv = np.float32(1) / np.float32(10000) ** (np.arange(0, dim, 2, dtype=np.float32) / np.float32(dim))
        f = np.arange(length, dtype=np.float32)[:, None] * inv.astype(np.float32)[None]
        return np.repeat(np.sin(f), 2, -1).astype(np.float32), np.repeat(np.cos(f), 2, -1).astype(np.float32)

    sin, cos = table(L, DC)
    rk = np.zeros((P, 2, LC, DC), np.float32)
    sgn = np.where(np.arange(DC) < DC // 2, -1, 1).astype(np.float32)
    pad = np.zeros((LPAD - L, DC), np.float32)
    rk[:, 0] = np.concatenate([cos, pad]).reshape(LC, P, DC).transpose(1, 0, 2)
    rk[:, 1] = np.concatenate([sin * sgn, pad]).reshape(LC, P, DC).transpose(1, 0, 2)
    sin, cos = table(S, DQ)
    ct, st = cos.T.reshape(2, QC // 2, P, S), sin.T.reshape(2, QC // 2, P, S)
    rq = np.zeros((P, 2, 2, QC // 2, S), np.float32)
    rq[:, 0] = ct.transpose(2, 0, 1, 3)
    rq[:, 1, 0] = st[1].transpose(1, 0, 2)
    rq[:, 1, 1] = -st[0].transpose(1, 0, 2)
    return {"consts": c, "ropek": rk.reshape(P, -1), "ropeq": rq.reshape(P, -1)}


class Plan:

    def __init__(self, nc, base, limit):
        self.nc, self.at, self.limit, self.n = nc, base, limit, 0

    def put(self, name, shape, dt=F32):
        size = int(np.prod(shape[1:])) * (2 if dt == F16 else 4)
        t = self.nc.alloc_sbuf_tensor_at(f"{name}_{self.at}", list(shape), dt, offset=self.at)
        self.at += -(-size // 32) * 32
        assert self.at <= self.limit, (name, self.at, self.limit)
        return t

    def here(self):
        return Plan(self.nc, self.at, self.limit)


def build(nc, A, stages=("a0", "moe", "a1", "ffn")):
    ctx = ExitStack()
    with ctx:
        sems = {}

        def sem(name):
            if name not in sems:
                sems[name] = ctx.enter_context(nc.semaphore(name))
            return sems[name]

        slab = nc.sbuf_bytes_remaining // 32 * 32 - 64
        arena = ctx.enter_context(nc.sbuf_tensor("arena", [P, slab // 4], F32))
        base = nc.sbuf_usable_end - nc.sbuf_bytes_remaining - slab
        base = -(-base // 32) * 32
        plan = Plan(nc, base, nc.sbuf_usable_end)
        PS = ctx.enter_context(nc.psum_tensor("PS", [P, 8, 512], F32))

        X = plan.put("X", [P, MT, D])
        cst = plan.put("cst", [P, C_N])
        bn = plan.put("bn", [P, MT, 2, 6])
        mv = plan.put("mv", [P, MT, 2])
        ve = plan.put("ve", [P, MT])
        sd = plan.put("sd", [P, MT])
        rstd = plan.put("rstd", [P, MT])
        absum = plan.put("absum", [P, 24])
        abpart = plan.put("abpart", [P, 24])
        ident, ones, tri = cst[:, C_ID:C_ID + P], cst[:, C_ONE:C_ONE + P], cst[:, C_TRI:C_TRI + P]

        pa = plan.here()
        xnT = pa.put("xnT", [P, KC, T])
        wq_h = [pa.put(f"wq_h{i}", [P, WQ_N]) for i in range(2)]
        wc_h = [pa.put(f"wc_h{i}", [P, WC_N]) for i in range(2)]
        pab = pa.here()
        absin = [pab.put("absin", [P, D])]
        ropeq = pa.put("ropeq", [P, 2, 2, QC // 2, S])
        assert pab.at <= pa.at
        mx = pa.put("mx", [P, GW])
        diag = pa.put("diag", [P, HA, S])
        sums = pa.put("sums", [P, GW])
        rz = pa.put("rz", [P, GW])
        nmx = pa.put("nmx", [P, HA])
        hn = [pa.put(f"hn{i}", [P, D]) for i in range(2)]
        absin.append(hn[1])
        tail = hn[0]
        pshare = pa.here()
        pa_sb = pa.here()
        Sb = [pa_sb.put(f"Sb{i}", [P, LC, GW]) for i in range(3)]
        pctx = pshare.here()
        pctx.at += 4 * HA * T
        ctxl = pctx.put("ctxl", [P, HA, T])
        assert pctx.at <= pa_sb.at
        pl0, pl1 = pshare.here(), pshare.here()
        qhk = [pl0.put(f"qhk{i}", [P, T]) for i in range(2)]
        rt = [[pl0.put(f"rt{i}{j}", [P, 2, HALF]) for j in range(2)] for i in range(2)]
        qrope = [pl0.put(f"qrope{i}", [P, 2, HALF]) for i in range(4)]
        qr = [pl0.put(f"qr{i}", [P, HALF]) for i in range(2)]
        mT_sb = pl1.put("mT_sb", [P, K])
        m_sb = pl1.put("m_sb", [P, 2 * R])
        aT_sb = pl1.put("aT_sb", [P, D])
        a_sb = pl1.put("a_sb", [P, KC, P])
        qr1 = [pl1.put("qr10", [P, T])]
        pl1.at = max(pl1.at, pa_sb.at)
        qr1.append(pl1.put("qr11", [P, T]))
        wk = pl1.put("wk", [P, HA, DC])
        pa.at = max(pa_sb.at, pl0.at, pl1.at)
        qc = pa.put("qc", [P, CC, B, GW])
        pprep = pa.here()
        kvT = [pa.put(f"kvT{i}", [P, CC, LPAD]) for i in range(2)]
        kvN = [pa.put(f"kvN{i}", [P, LC, DC]) for i in range(3)]
        wb = pa.put("wb", [P, WB_N])
        ropek = pprep.put("ropek", [P, 2, LC, DC])
        cin = [pprep.put(f"cin{i}", [P, LC, DC]) for i in range(2)]
        crot = [pprep.put(f"crot{i}", [P, 2, DC]) for i in range(2)]
        crope = [pprep.put(f"crope{i}", [P, LC, DC]) for i in range(2)]
        cT = pprep.put("cT", [P, CC, LPAD])

        kvT_d = nc.dram_tensor("kvT_d", [B, P, CC * LPAD], F32, kind="Internal").ap()
        kvN_d = nc.dram_tensor("kvN_d", [B, P, LC * DC], F32, kind="Internal").ap()
        h_d = nc.dram_tensor("h_d", [TPAD, D], F32, kind="Internal").ap()
        y_d = nc.dram_tensor("y_d", [max(MAX_PAIRS * 2, E + HG * FILL) * P, D], F32, kind="Internal").ap()

        pm = plan.here()
        W2 = pm.put("W2", [P, 2, W2_N])
        bias2 = pm.put("bias2", [P, 2, 2 * FI])
        lg = pm.put("lg", [P, MT, E])
        sel = pm.put("sel", [P, MT, E])
        eq = pm.put("eq", [P, MT, E])
        csc = pm.put("csc", [P, MT, E])
        ex = pm.put("ex", [P, MT, E])
        Gt = pm.put("Gt", [P, MT, E])
        pos = pm.put("pos", [P, MT, E])
        eqk = [pm.put(f"eqk{i}", [P, MT, E]) for i in range(TOPK)]
        v8 = pm.put("v8", [P, MT, 8])
        need = pm.put("need", [P, MT])
        ssum = pm.put("ssum", [P, MT])
        nt = pm.put("nt", [P, E])
        tend = pm.put("tend", [P, E])
        tst = pm.put("tst", [P, E])
        cnt = pm.put("cnt", [P, E])
        te_c = pm.put("te_c", [P, 1])
        slot = pm.put("slot", [P, TOPK, MT])
        Gk = pm.put("Gk", [P, TOPK, MT])
        slot_i = pm.put("slot_i", [P, TOPK * MT], I32)
        srow_i = pm.put("srow_i", [P, TOPK * MT], I32)
        srow = pm.put("srow", [P, TOPK * MT])
        sbase = pm.put("sbase", [P, TOPK * MT])
        idx = pm.put("idx", [P, IDXW], I32)
        idxc = [pm.put(f"idxc{i}", [P, 1], I32) for i in range(2)]
        te_f = pm.put("te_f", [P, IDXW])
        te_i = pm.put("te_i", [P, IDXW], I32)
        tp_i = pm.put("tp_i", [P, IDXW], I32)
        te2_i = pm.put("te2_i", [P, E], I32)
        te_end = pm.put("te_end", [P, E], I32)
        np_i = pm.put("np_i", [P, 4], I32)
        te_odd = [pm.put(f"te_odd{q}", [P, E], I32) for q in range(2)]
        gwT = pm.put("gwT", [P, KC, E])
        gb = pm.put("gb", [P, E])
        bd_room = pm.put("bd", [P, D])
        bd = bd_room[0:E, :]
        GT = pm.put("GT", [E, TPAD])
        hnm = [pm.put(f"hnm{i}", [P, D]) for i in range(2)]
        pr, pt = pm.here(), pm.here()
        hTm = pr.put("hTm", [P, KC, TPAD])
        lgT = pr.put("lgT", [P, TPAD])
        oh_s = pr.put("oh_s", [P, TOPK * MT, P], F16)
        oh_j = pr.put("oh_j", [P, 4, MAX_TILES], F16)
        hs = [pt.put(f"hs{i}", [P, D]) for i in range(2)]
        hT2 = [pt.put(f"hT2{i}", [P, KC, P]) for i in range(2)]
        gl = pt.put("gl", [P, FI])
        sg = pt.put("sg", [P, FI])
        up1 = pt.put("up1", [P, FI])
        act = [pt.put(f"act{i}", [P, FI]) for i in range(2)]
        actT = pt.put("actT", [P, IC, P])
        ysb = [pt.put(f"ysb{i}", [P, D]) for i in range(2)]
        yg = [pt.put("yg", [P, D]), bd_room] + hnm + hs

        pf = plan.here()
        xh = [pf.put(f"xh{i}", [P, KC, T], F16) for i in range(2)]
        stg = [pf.put(f"stg{i}", [P, 3, D]) for i in range(2)]
        gtq = [pf.put(f"gtq{i}", [P, 3, D], F16) for i in range(2)]
        wq = [pf.put(f"wq{i}", [P, 2, KC, P], F16) for i in range(2)]
        wdq = pf.put("wdq", [P, EB, D], F16)
        sgf = [pf.put(f"sgf{i}", [P, 2, HALF]) for i in range(2)]
        hid = [pf.put(f"hid{i}", [P, 2, HALF]) for i in range(2)]
        tern = pf.put("tern", [P, 3])
        tsum = pf.put("tsum", [P, 3])
        thr = pf.put("thr", [P, 3])
        nthr = pf.put("nthr", [P, 3])
        upsc = pf.put("upsc", [P, 1])
        cd1 = pf.put("cd1", [P, 1])
        cd2 = pf.put("cd2", [P, 1])
        phn = pf.here()
        hnf = [phn.put(f"hnf{i}", [P, D]) for i in range(2)]
        hh = [pf.put(f"hh{i}", [P, EB, T], F16) for i in range(2)]
        tailf = pf.put("tailf", [P, D])

        NSTAT = 2 * MT - 2
        NK, NPOOL = TOPK * MT, KPOOL * MT
        x_t = A["x"]
        out_t = A["out"]
        HN = {"a0": hn, "moe": hnm, "a1": hn, "ffn": hnf}
        block = ctx.enter_context(nc.Block())

        def ln_count(p, what, n):
            each = {"var": 2, "sd": 1, "agg": MT, "hn": MT, "tp": 2 * MT, "ev": 2 * MT}[what]
            return each * ("a0", "moe", "a1", "ffn").index(p) + n

        def statistics(m, j, done):
            nc.vector.bn_stats(bn[:, m, j, :], X[:, m, j * 512:(j + 1) * 512]).then_inc(sem(done), 1)

        def ln_vector(dve, p, taken):
            dve.wait_ge(sem(taken[0]), taken[1])
            for m in range(MT):
                nc.vector.bn_aggr(mv[:, m, :], bn[:, m, :, :]).then_inc(sem("ln_agg"), 1)
            dve.wait_ge(sem("ln_agg"), ln_count(p, "agg", MT))
            nc.vector.tensor_scalar(ve[:, :], mv[:, :, 1], EPS, None, ALU.add).then_inc(sem("ln_var"), 1)
            dve.wait_ge(sem("ln_sd"), ln_count(p, "sd", 1))
            nc.vector.reciprocal(rstd[:, :], sd[:, :]).then_inc(sem("ln_var"), 1)
            dve.wait_ge(sem("ln_var"), ln_count(p, "var", 2))

        def ln_tile(dve, p, m, stored=False):
            if m >= 2:
                dve.wait_ge(sem("ln_tp"), ln_count(p, "tp", 2 * (m - 1)))
                if stored:
                    dve.wait_ge(sem(f"{p}_st{m % 2}"), 16 * (m // 2))
            nc.vector.tensor_scalar(HN[p][m % 2][:, :], X[:, m, :], mv[:, m, 0:1], rstd[:, m:m + 1],
                                    ALU.subtract, ALU.mult).then_inc(sem("ln_hn"), 1)

        def ln_tensor(pe, p, then=None):
            for m in range(MT):
                pe.wait_ge(sem("ln_hn"), ln_count(p, "hn", m + 1))
                for h in range(2):
                    if m >= 2:
                        pe.wait_ge(sem("ln_ev"), ln_count(p, "ev", 2 * (m - 2) + h + 1))
                    for c in range(4):
                        mm = nc.tensor.transpose(PS[:, 2 * (m % 2) + h, c * P:(c + 1) * P],
                                                 HN[p][m % 2][:, (4 * h + c) * P:(4 * h + c + 1) * P], ident)
                    mm.then_inc(sem("ln_tp"), 1)
                if then and m >= 1:
                    then(m - 1)
            if then:
                then(MT - 1)

        def ln_scalar(eng, p, dst, pad=False):
            eng.wait_ge(sem("ln_var"), ln_count(p, "var", 1))
            nc.scalar.activation(sd[:, :], ve[:, :], ACT.Sqrt).then_inc(sem("ln_sd"), 1)
            for m in range(MT):
                w = P if pad else TW[m]
                for h in range(2):
                    eng.wait_ge(sem("ln_tp"), ln_count(p, "tp", 2 * m + h + 1))
                    src = PS[:, 2 * (m % 2) + h, :].rearrange("p (c t) -> p c t", c=4)[:, :, 0:w]
                    if dst is xh:
                        nc.scalar.activation(xh[0][:, 4 * h:4 * h + 4, m * P:m * P + w], src, ACT.Copy,
                                             scale=XS).then_inc(sem(f"{p}_hi"), 1)
                    else:
                        nc.scalar.activation(dst[:, 4 * h:4 * h + 4, m * P:m * P + w], src,
                                             ACT.Copy).then_inc(sem("ln_ev"), 1)

        def prep_sync(sp):
            for m in range(MT):
                if m == MT - 1:
                    sp.wait_ge(sem("x_zero"), 1)
                sp.dma_start(X[0:TW[m], m, :], x_t[m * P:m * P + TW[m], :]).then_inc(sem(f"x_in{m // 2}"), 16)
            sp.dma_start(cst[:, :], A["consts"]).then_inc(sem("cst_in"), 16)
            sp.dma_start(ropeq[:, :, :, :, :], A["ropeq"].rearrange("p (a i c s) -> p a i c s", a=2, i=2, c=QC // 2)).then_inc(sem("rope_in"), 16)

        def prep_first(sp):
            sp.dma_start(ropek[:, :, :, :], A["ropek"].rearrange("p (a c d) -> p a c d", a=2, c=LC)).then_inc(sem("rope_in"), 16)

        def prep_load(pool, b):
            src = A["ctx"][b]
            pool.dma_start(cin[b % 2][:, 0:LC - 1, :], src[0:(LC - 1) * P, :].rearrange("(c p) d -> p c d", p=P)).then_inc(sem(f"cin{b % 2}"), 16)
            pool.dma_start(cin[b % 2][0:LREST, LC - 1, :], src[(LC - 1) * P:L, :]).then_inc(sem(f"cin{b % 2}"), 16)

        def prep_zero(pool):
            nc.gpsimd.memset(X[:, MT - 1, :], 0.0).then_inc(sem("x_zero"), 1)
            for i in range(2):
                nc.gpsimd.memset(cin[i][:, LC - 1, :], 0.0).then_inc(sem("cin_zero"), 1)
            pool.wait_ge(sem("cin_zero"), 2)
            for b in range(2):
                prep_load(pool, b)

        def prep_add(dve, k):
            b, rows = k // 3, slice(2 * (k % 3), 2 * (k % 3) + 2)
            dve.wait_ge(sem("crot_done"), k + 1)
            dve.wait_ge(sem("ccos_done"), k + 1)
            nc.vector.tensor_tensor(crope[b % 2][:, rows, :], crope[b % 2][:, rows, :], crot[k % 2][:, :, :],
                                    ALU.add).then_inc(sem("c_rope"), 1)

        def prep_vector(dve, k):
            b, rows = k // 3, slice(2 * (k % 3), 2 * (k % 3) + 2)
            if k == 0:
                dve.wait_ge(sem("rope_in"), 32)
            if k % 3 == 0:
                dve.wait_ge(sem(f"cin{b % 2}"), 32 * (b // 2 + 1))
                if b >= 2:
                    dve.wait_ge(sem(f"cn_out{b % 2}"), 16 * (b // 2))
                    dve.wait_ge(sem("c_tp"), 3 * (b - 1))
            nc.vector.tensor_tensor(crope[b % 2][:, rows, :], cin[b % 2][:, rows, :], ropek[:, 0, rows, :],
                                    ALU.mult).then_inc(sem("ccos_done"), 1)
            if k >= 1:
                prep_add(dve, k - 1)

        def prep_pool(pool, k):
            b, rows, hd = k // 3, slice(2 * (k % 3), 2 * (k % 3) + 2), DC // 2
            if k == 0:
                pool.wait_ge(sem("rope_in"), 32)
            if k % 3 == 0:
                pool.wait_ge(sem(f"cin{b % 2}"), 32 * (b // 2 + 1))
                if 1 <= b < B - 1:
                    pool.wait_ge(sem("ccos_done"), 3 * b)
                    pool.wait_ge(sem("crot_done"), 3 * b)
                    prep_load(pool, b + 1)
            if k >= 2:
                pool.wait_ge(sem("c_rope"), k - 1)
            nc.gpsimd.tensor_tensor(crot[k % 2][:, :, 0:hd], cin[b % 2][:, rows, hd:DC], ropek[:, 1, rows, 0:hd], ALU.mult)
            nc.gpsimd.tensor_tensor(crot[k % 2][:, :, hd:DC], cin[b % 2][:, rows, 0:hd], ropek[:, 1, rows, hd:DC],
                                    ALU.mult).then_inc(sem("crot_done"), 1)

        def prep_tensor(pe, k):
            pe.wait_ge(sem("c_rope"), k + 1)
            if k >= 1:
                pe.wait_ge(sem("c_ev"), k)
            for dc in range(CC):
                for r in range(2):
                    mm = nc.tensor.transpose(PS[:, 1, (2 * dc + r) * P:(2 * dc + r + 1) * P],
                                             crope[k // 3 % 2][:, 2 * (k % 3) + r, dc * P:(dc + 1) * P], ident)
            mm.then_inc(sem("c_tp"), 1)

        def prep_scalar(eng, k):
            b, j = k // 3, k % 3
            if b >= 1 and j == 0:
                eng.wait_ge(sem("ct_out"), 16 * b)
            eng.wait_ge(sem("c_tp"), k + 1)
            nc.scalar.activation(cT[:, :, 2 * j * P:(2 * j + 2) * P], PS[:, 1, :].rearrange("p (c l) -> p c l", c=CC),
                                 ACT.Copy).then_inc(sem("c_ev"), 1)
            if j == 2:
                eng.dma_start(kvN_d[b], crope[b % 2][:, :, :].rearrange("p c d -> p (c d)")).then_inc(sem(f"cn_out{b % 2}"), 16)
                eng.wait_ge(sem("c_ev"), k + 1)
                eng.dma_start(kvT_d[b], cT[:, :, :].rearrange("p c l -> p (c l)")).then_inc(sem("ct_out"), 16)

        def att_sync(sp, ly):
            p, WQ, WC, WB, g0 = "a", A[f"WQ{ly}"], A[f"WC{ly}"], A[f"WB{ly}"], ly * HG
            if ly == 1:
                sp.wait_ge(sem("m_add"), NK - NPOOL)

            def head_q(h, slot):
                sp.dma_start(wq_h[slot][:, :], WQ[h - HA * g0]).then_inc(sem(f"{p}_wq{slot}"), 16)

            def head_c(h, slot):
                sp.dma_start(wc_h[slot][:, 0:WC_K], WC[h - HA * g0][:, 0:WC_K]).then_inc(sem(f"{p}_wc{slot}"), 16)

            def head_k(h, slot):
                sp.dma_start(wc_h[slot][:, WC_K:WC_N], WC[h - HA * g0][:, WC_K:WC_N]).then_inc(sem(f"{p}_wk{slot}"), 16)

            def kt(b):
                sp.dma_start(kvT[b % 2][:, :, :], kvT_d[b].rearrange("p (c l) -> p c l", c=CC)).then_inc(sem(f"{p}_kt{b % 2}"), 16)

            def kn(b):
                sp.dma_start(kvN[b % 3][:, :, :], kvN_d[b].rearrange("p (c d) -> p c d", c=LC)).then_inc(sem(f"{p}_kn{b % 3}"), 16)

            def group(g):
                sp.dma_start(wb[:, :], WB[g - g0]).then_inc(sem(f"{p}_wb"), 16)
                if ly == 1:
                    sp.dma_start(wk[:, :, :], A["WK"][g - g0].rearrange("p (a d) -> p a d", a=HA)).then_inc(sem(f"{p}_wk"), 16)

            def first_loads():
                for b in range(2):
                    kt(b)
                for b in range(3):
                    kn(b)
                group(g0)

            def body(hg, last, first=False):
                if ly == 0:
                    for part, a in (("q", 0), ("q", 1), ("c", 0), ("k", 0), ("q", 2), ("c", 1), ("k", 1), ("q", 3),
                                    ("c", 2), ("k", 2), ("c", 3)):
                        if last and a >= 2:
                            continue
                        if part == "q":
                            sp.wait_ge(sem(f"{p}_qh"), 8 * hg + 2 * (a + 1))
                            head_q(HA * hg + a + 2, a % 2)
                        elif part == "c":
                            sp.wait_ge(sem(f"{p}_qrm"), 12 * hg + 3 * (a + 1))
                            head_c(HA * hg + a + 2, a % 2)
                        else:
                            sp.wait_ge(sem(f"{p}_qc"), 16 * hg + 4 * (a + 1))
                            head_k(HA * hg + a + 2, a % 2)
                else:
                    for a in range(2 if last else HA):
                        sp.wait_ge(sem(f"{p}_f"), 12 * (hg - g0) + 6 * (a // 2) + 4)
                        head_c(HA * hg + a + 2, a % 2)
                        head_q(HA * hg + a + 2, a % 2)
                if first:
                    sp.wait_ge(sem("c_rope"), NQ)
                    sp.wait_ge(sem("ct_out"), 16 * (B - 1))
                    sp.wait_ge(sem("cn_out0"), 16 * (B // 2))
                    sp.wait_ge(sem("cn_out1"), 16 * (B // 2 - 1))
                    for b in range(2):
                        kt(b)
                    for b in range(2):
                        kn(b)
                    sp.wait_ge(sem("ct_out"), 16 * B)
                    sp.wait_ge(sem("cn_out1"), 16 * (B // 2))
                    kn(2)
                    group(0)
                for b in range(2, B):
                    if b == 3 and ly == 0 and not last:
                        sp.wait_ge(sem(f"{p}_qc"), 16 * hg + 16)
                        head_k(HA * hg + HA + 1, (HA - 1) % 2)
                    sp.wait_ge(sem(f"{p}_sc"), hg * LC * B + LC * (b - 1))
                    kt(b)
                    if b >= 3:
                        sp.wait_ge(sem(f"{p}_cx"), hg * 2 * B + 2 * (b - 2))
                        kn(b)
                if not last:
                    for b in range(2):
                        sp.wait_ge(sem(f"{p}_sc"), hg * LC * B + LC * (B - 1 + b))
                        kt(b)
                    for b, n in ((2, B - 2), (0, B - 1), (1, B)):
                        sp.wait_ge(sem(f"{p}_cx"), hg * 2 * B + 2 * n)
                        kn(b)
                    sp.wait_ge(sem(f"{p}_add"), (hg + 1) * 2 * MT)
                    group(hg + 1)

            for a in range(2):
                head_q(HA * g0 + a, a)
                head_c(HA * g0 + a, a)
                if ly == 0:
                    head_k(a, a)
            if ly == 0:
                prep_first(sp)
                body(0, False, first=True)
            else:
                first_loads()
            with sp.Fori(g0 + (ly == 0), g0 + HG - 1) as hg:
                body(hg, False)
            body(g0 + HG - 1, True)

        def qc_place(ly, a, i):
            if ly == 0 or a < HA - 2:
                return 4 * a + i
            return 4 * (HA - 2) + 4 * (i // 2) + 2 * (a - HA + 2) + i % 2

        def qc_bank(ly, a, i):
            return 6 + i % 2 if ly else (7, 1, 7, 6)[i] if a == HA - 1 else 7

        def att_tensor(pe, ly):
            p, g0 = "a", ly * HG
            n_ev = LC * B

            def q_heads(hg, a, half, cs):
                if cs[0] == 0:
                    if half == 0:
                        pe.wait_ge(sem(f"{p}_wq{a % 2}"), 32 * hg + 16 * (a // 2 + 1))
                    if a >= 1:
                        pe.wait_ge(sem(f"{p}_qhk"), 8 * hg + 2 * a + half)
                for c in cs:
                    mm = nc.tensor.matmul(PS[:, half if a == 0 else 0, 0:HALF], wq_h[a % 2][:, c * K:(c + 1) * K],
                                          xnT[:, c, half * HALF:(half + 1) * HALF], start=c == 0, stop=c == KC - 1)
                if cs[-1] == KC - 1:
                    mm.then_inc(sem(f"{p}_qh"), 1)

            def q_big(hg, a, s):
                c, half, k = s // 2, s % 2, 6 * a + s
                if s == 0:
                    pe.wait_ge(sem(f"{p}_wc{a % 2}"), 32 * hg + 16 * (a // 2 + 1))
                pe.wait_ge(sem(f"{p}_qhk"), 8 * hg + 2 * a + half + 1)
                if k >= 2:
                    pe.wait_ge(sem(f"{p}_rt"), NQ * hg + k - 1)
                for i in range(2):
                    w = WC_C + (c + 3 * i) * P
                    mm = nc.tensor.matmul(PS[:, 2 + 2 * (k % 2) + i, 0:HALF], wc_h[a % 2][:, w:w + P],
                                          qhk[a % 2][:, half * HALF:(half + 1) * HALF], start=True, stop=True)
                mm.then_inc(sem(f"{p}_qb"), 1)

            def q_r(hg, a, c):
                pe.wait_ge(sem(f"{p}_rope"), NQ * hg + 6 * a + 2 * c + 2)
                if c == 0 and a > 0:
                    pe.wait_ge(sem(f"{p}_qre"), HA * hg + a)
                for i in range(2):
                    w = WC_R + (c + 3 * i) * R
                    for half in range(2):
                        mm = nc.tensor.matmul(PS[half * R:(half + 1) * R, 6, 0:HALF], wc_h[a % 2][:, w:w + R],
                                              qrope[(6 * a + 2 * c + half) % 4][:, i, :],
                                              start=c == 0 and i == 0, stop=c == 2 and i == 1)
                mm.then_inc(sem(f"{p}_qrm"), 1)

            def q_c0(hg, a, i):
                half, dc = i // 2, i % 2
                if i == 0:
                    pe.wait_ge(sem(f"{p}_wk{a % 2}"), 32 * hg + 16 * (a // 2 + 1))
                pe.wait_ge(sem(f"{p}_qre"), HA * hg + a + 1)
                bank = qc_bank(0, a, i)
                if bank == 7 and 4 * a + i > 0:
                    before_it = 4 * a + i - (2 if a == HA - 1 and i == 2 else 1)
                    pe.wait_ge(sem(f"{p}_qce"), 16 * hg + before_it + 1)
                w = WC_K + half * DC + dc * P
                nc.tensor.matmul(PS[:, bank, 0:HALF], wc_h[a % 2][:, w:w + P], qr[a % 2][:, :],
                                 start=True, stop=True).then_inc(sem(f"{p}_qc"), 1)

            def fold_done(hg, u, n):
                pe.wait_ge(sem(f"{p}_fe"), 12 * (hg - g0) + 6 * u + n)

            def fold_m(hg, u):
                for j in range(2):
                    pe.wait_ge(sem(f"{p}_wc{j}"), 32 * hg + 16 * (u + 1))
                for c in range(QC):
                    for j in range(2):
                        mm = nc.tensor.matmul(PS[j * R:(j + 1) * R, 1, 0:K], wc_h[j][:, WC_R + c * R:WC_R + (c + 1) * R],
                                              wc_h[j][:, WC_C + c * K:WC_C + (c + 1) * K], start=c == 0, stop=c == QC - 1)
                mm.then_inc(sem(f"{p}_f"), 1)

            def fold_mt(hg, u):
                fold_done(hg, u, 1)
                nc.tensor.transpose(PS[:, 3, 0:P], mT_sb[:, :], ident).then_inc(sem(f"{p}_f"), 1)

            def fold_a(hg, u):
                for j in range(2):
                    pe.wait_ge(sem(f"{p}_wq{j}"), 32 * hg + 16 * (u + 1))
                fold_done(hg, u, 2)
                for nh in range(2):
                    for j in range(2):
                        mm = nc.tensor.matmul(PS[j * R:(j + 1) * R, 4 + nh, :], m_sb[:, j * R:(j + 1) * R],
                                              wq_h[j][:, nh * 512:(nh + 1) * 512], start=True, stop=True)
                    mm.then_inc(sem(f"{p}_f"), 1)

            def fold_at(hg, u):
                for nh in range(2):
                    fold_done(hg, u, 3 + nh)
                    for c in range(4):
                        cc = 4 * nh + c
                        mm = nc.tensor.transpose(PS[:, 2 + nh, c * P:(c + 1) * P], aT_sb[:, cc * P:(cc + 1) * P], ident)
                    mm.then_inc(sem(f"{p}_f"), 1)

            def q_r1(hg, u):
                fold_done(hg, u, 6)
                for half in range(2):
                    if u:
                        pe.wait_ge(sem(f"{p}_q1e"), 4 * (hg - g0) + half + 1)
                    for c in range(KC):
                        mm = nc.tensor.matmul(PS[:, half, 0:HALF], a_sb[:, c, :],
                                              xnT[:, c, half * HALF:(half + 1) * HALF], start=c == 0, stop=c == KC - 1)
                    mm.then_inc(sem(f"{p}_q1"), 1)

            def q_c1(hg, a, i):
                half, dc, n = i // 2, i % 2, qc_place(1, a, i)
                pe.wait_ge(sem(f"{p}_wk"), 16 * (hg - g0 + 1))
                pe.wait_ge(sem(f"{p}_q1e"), 4 * (hg - g0) + 2 * (a // 2) + half + 1)
                if n >= 2:
                    pe.wait_ge(sem(f"{p}_qce"), 16 * hg + n - 1)
                nc.tensor.matmul(PS[:, 6 + i % 2, 0:HALF], wk[:, a, dc * P:(dc + 1) * P],
                                 qr1[a // 2][:, half * HALF:(half + 1) * HALF], start=True, stop=True).then_inc(sem(f"{p}_qc"), 1)

            def scores(hg, b, lcs):
                for lc in lcs:
                    n = LC * b + lc
                    if n >= 3:
                        pe.wait_ge(sem(f"{p}_se"), n_ev * hg + n - 2)
                    for dc in range(CC):
                        mm = nc.tensor.matmul(PS[:, lc % 3, 0:GW], kvT[b % 2][:, dc, lc * P:(lc + 1) * P],
                                              qc[:, dc, b, :], start=dc == 0, stop=dc == CC - 1)
                    mm.then_inc(sem(f"{p}_sc"), 1)

            def values(hg, b, dc):
                if dc == 0:
                    pe.wait_ge(sem(f"{p}_ex"), B * hg + b + 1)
                    pe.wait_ge(sem(f"{p}_kn{b % 3}"), 16 * ((3, 3, 2)[b % 3] * hg + b // 3 + 1))
                    if b >= 1:
                        pe.wait_ge(sem(f"{p}_cxe"), B * hg + b)
                    else:
                        pe.wait_ge(sem(f"{p}_qce"), 16 * hg + 16)
                for lc in range(LC):
                    k = P if lc < LC - 1 else LREST
                    mm = nc.tensor.matmul(PS[:, 6 + dc, 0:GW], kvN[b % 3][0:k, lc, dc * P:(dc + 1) * P],
                                          Sb[b % 3][0:k, lc, :], start=lc == 0, stop=lc == LC - 1)
                mm.then_inc(sem(f"{p}_cx"), 1)

            def softmax_sum(hg, b):
                pe.wait_ge(sem(f"{p}_sum"), B * hg + b + 1)
                nc.tensor.matmul(PS[:, 5, 0:GW], ones, sums[:, :], start=True, stop=True).then_inc(sem(f"{p}_z"), 1)

            def q_late(hg, n):
                if ly == 0:
                    q_c0(hg, HA - 1, 2 + n)
                else:
                    for i in (2, 3):
                        q_c1(hg, HA - 2 + n, i)

            def next_group(hg, n):
                if ly == 0:
                    q_heads(hg, 0, n, range(KC))
                elif n == 0:
                    fold_m(hg, 0)

            def body(hg, first=False):
                if ly == 0:
                    if first:
                        for half in range(2):
                            q_heads(hg, 0, half, range(KC))
                    for a in range(HA):
                        for s in range(6):
                            q_big(hg, a, s)
                            if a < HA - 1:
                                q_heads(hg, a + 1, s // 3, (range(0, 3), range(3, 6), range(6, KC))[s % 3])
                            if s == 1 and a >= 1:
                                q_r(hg, a - 1, 2)
                            if s == 3 or s == 5:
                                q_r(hg, a, s // 2 - 1)
                            if s >= 2 and a >= 1:
                                q_c0(hg, a - 1, s - 2)
                            if first and 6 * a + s >= 2:
                                prep_tensor(pe, 6 * a + s - 2)
                    if first:
                        prep_tensor(pe, NQ - 2)
                    q_r(hg, HA - 1, 2)
                    if first:
                        prep_tensor(pe, NQ - 1)
                        pe.wait_ge(sem("c_ev"), NQ)
                    for i in range(2):
                        q_c0(hg, HA - 1, i)
                else:
                    fold_mt(hg, 0)
                    fold_a(hg, 0)
                    fold_at(hg, 0)
                    q_r1(hg, 0)
                    for i in range(4):
                        q_c1(hg, 0, i)
                    fold_m(hg, 1)
                    for i in range(2):
                        q_c1(hg, 1, i)
                    fold_mt(hg, 1)
                    for i in range(2, 4):
                        q_c1(hg, 1, i)
                    fold_a(hg, 1)
                    fold_at(hg, 1)
                    q_r1(hg, 1)
                    for a in range(2, HA):
                        for i in range(2):
                            q_c1(hg, a, i)
                n_late = 2 if ly == 0 else 4
                pe.wait_ge(sem(f"{p}_qce"), 16 * hg + 16 - n_late)
                for st in range(B + 2):
                    if st < B:
                        pe.wait_ge(sem(f"{p}_kt{st % 2}"), 16 * (4 * hg + st // 2 + 1))
                        scores(hg, st, range(0, 3))
                    if st == 1:
                        q_late(hg, 0)
                    if 1 <= st <= B:
                        pe.wait_ge(sem(f"{p}_mx"), B * hg + st)
                        for a in range(HA):
                            mm = nc.tensor.transpose(PS[0:S, 3, a * P:(a + 1) * P], mx[:, a * S:(a + 1) * S], ident)
                        mm.then_inc(sem(f"{p}_mt"), 1)
                    if st < B:
                        scores(hg, st, range(3, LC))
                    if st == 1:
                        q_late(hg, 1)
                    if st >= B:
                        if first:
                            next_group(hg + 1, st - B)
                        else:
                            with pe.If(hg < g0 + HG - 1):
                                next_group(hg + 1, st - B)
                    if 1 <= st <= B:
                        pe.wait_ge(sem(f"{p}_dg"), B * hg + st)
                        nc.tensor.matmul(PS[:, 4, 0:GW], ones[0:S, :], diag[0:S, :, :].rearrange("p a s -> p (a s)"),
                                         start=True, stop=True).then_inc(sem(f"{p}_mb"), 1)
                    if st >= 2:
                        softmax_sum(hg, st - 2)
                        for dc in range(CC):
                            values(hg, st - 2, dc)
                pe.wait_ge(sem(f"{p}_wb"), 16 * (hg + 1))
                for n in range(2 * HA):
                    half, a = n // HA, n % HA
                    if a == 0:
                        pe.wait_ge(sem(f"{p}_cxe"), B * hg + (B if half else B - 1))
                    if n >= 2:
                        pe.wait_ge(sem(f"{p}_lte"), 8 * hg + n - 1)
                    for dc in range(CC):
                        w = WB_V + (a * CC + dc) * K
                        rhs = qc[:, dc, half * BH:(half + 1) * BH, a * S:(a + 1) * S]
                        mm = nc.tensor.matmul(PS[:, 3 + n % 2, 0:HALF], wb[:, w:w + K], rhs, start=dc == 0, stop=dc == CC - 1)
                    mm.then_inc(sem(f"{p}_lt"), 1)
                pe.wait_ge(sem(f"{p}_lte"), 8 * hg + 8)
                for n in range(2 * MT):
                    m, nh = n // 2, n % 2
                    if n >= 4:
                        pe.wait_ge(sem(f"{p}_add"), 2 * MT * hg + n - 3)
                    for a in range(HA):
                        w = WB_O + a * D + nh * 512
                        if m < MT - 1:
                            mm = nc.tensor.matmul(PS[:, 2 + n % 4, :], ctxl[:, a, m * P:(m + 1) * P], wb[:, w:w + 512],
                                                  start=a == 0, stop=a == HA - 1)
                        else:
                            mm = nc.tensor.matmul(PS[a * TW[m]:(a + 1) * TW[m], 2 + n % 4, :], ctxl[:, a, m * P:T], wb[:, w:w + 512],
                                                  start=True, stop=True)
                    mm.then_inc(sem(f"{p}_op"), 1)
                pe.wait_ge(sem(f"{p}_add"), 2 * MT * (hg + 1))

            if ly == 0:
                body(0, first=True)
            else:
                fold_m(g0, 0)
            with pe.Fori(g0 + (ly == 0), g0 + HG) as hg:
                body(hg)
            for nh in range(2):
                nc.tensor.matmul(PS[0:TW[-1], 2 + nh, :], cst[:, C_FOLD:C_FOLD + TW[-1]], tail[:, nh * 512:(nh + 1) * 512],
                                 start=True, stop=True).then_inc(sem("a_fold"), 1)

        def att_scalar(eng, ly):
            p, g0 = "a", ly * HG
            n_ab = 24

            def copy(dst, src, s_in, v, s_out):
                eng.wait_ge(sem(f"{p}_{s_in}"), v)
                nc.scalar.activation(dst, src, ACT.Copy).then_inc(sem(f"{p}_{s_out}"), 1)

            def c_qhk(hg, a, half):
                copy(qhk[a % 2][:, half * HALF:(half + 1) * HALF], PS[:, half if a == 0 else 0, 0:HALF], "qh", 8 * hg + 2 * a + half + 1, "qhk")

            def c_qr(hg, a):
                copy(qr[a % 2][:, :], PS[:, 6, 0:HALF], "qrm", 12 * hg + 3 * a + 3, "qre")

            def c_qc(hg, a, i):
                half, dc = i // 2, i % 2
                copy(qc[:, dc, half * BH:(half + 1) * BH, a * S:(a + 1) * S],
                     PS[:, qc_bank(ly, a, i), 0:HALF].rearrange("p (b s) -> p b s", b=BH), "qc", 16 * hg + qc_place(ly, a, i) + 1, "qce")

            def fold(hg, u, n):
                dst, src = ((mT_sb[:, :], PS[:, 1, 0:K]), (m_sb[:, :], PS[:, 3, 0:P]),
                            (aT_sb[:, 0:512], PS[:, 4, :]), (aT_sb[:, 512:D], PS[:, 5, :]),
                            (a_sb[:, 0:4, :].rearrange("p c r -> p (c r)"), PS[:, 2, :]),
                            (a_sb[:, 4:KC, :].rearrange("p c r -> p (c r)"), PS[:, 3, :]))[n]
                copy(dst, src, "f", 12 * (hg - g0) + 6 * u + n + 1, "fe")

            def c_qr1(hg, u):
                for half in range(2):
                    copy(qr1[u][:, half * HALF:(half + 1) * HALF], PS[:, half, 0:HALF], "q1", 4 * (hg - g0) + 2 * u + half + 1, "q1e")

            def absolute(hg, k):
                eng.wait_ge(sem(f"ab_in{k % 2}"), 16 * (12 * (hg - g0) + k // 2 + 1))
                nc.scalar.activation(absin[k % 2][:, :], absin[k % 2][:, :], ACT.Abs,
                                     accum_out=abpart[:, k:k + 1]).then_inc(sem("ab_done"), 1)

            def late(n):
                return [(HA - 1, 2 + n)] if ly == 0 else [(HA - 2 + n, 2), (HA - 2 + n, 3)]

            def body(hg, first=False):
                if ly == 0:
                    for half in range(2):
                        c_qhk(hg, 0, half)
                    for a in range(HA):
                        for s in range(6):
                            if a < HA - 1 and s % 3 == 2:
                                c_qhk(hg, a + 1, s // 3)
                            if s == 1 and a >= 1:
                                c_qr(hg, a - 1)
                            if s >= 2 and a >= 1:
                                c_qc(hg, a - 1, s - 2)
                            if first and 6 * a + s >= 2:
                                prep_scalar(eng, 6 * a + s - 2)
                    if first:
                        prep_scalar(eng, NQ - 2)
                    c_qr(hg, HA - 1)
                    if first:
                        prep_scalar(eng, NQ - 1)
                    for i in range(2):
                        c_qc(hg, HA - 1, i)
                else:
                    for n in range(6):
                        fold(hg, 0, n)
                    c_qr1(hg, 0)
                    for i in range(4):
                        c_qc(hg, 0, i)
                    fold(hg, 1, 0)
                    for i in range(2):
                        c_qc(hg, 1, i)
                    fold(hg, 1, 1)
                    for i in range(2, 4):
                        c_qc(hg, 1, i)
                    for n in range(2, 6):
                        fold(hg, 1, n)
                    c_qr1(hg, 1)
                    for a in range(2, HA):
                        for i in range(2):
                            c_qc(hg, a, i)
                for st in range(B + 1):
                    if st < B:
                        for lc in range(LC):
                            n = LC * st + lc
                            eng.wait_ge(sem(f"{p}_sc"), LC * B * hg + n + 1)
                            bias = cst[:, C_PAD:C_PAD + 1] if lc == LC - 1 else 0.0
                            nc.scalar.activation(Sb[st % 3][:, lc, :], PS[:, lc % 3, 0:GW], ACT.Identity,
                                                 bias=bias).then_inc(sem(f"{p}_se"), 1)
                            if st == 1 and lc % 3 == 2:
                                for i in late(lc // 3):
                                    c_qc(hg, *i)
                            if ly == 1 and lc in (1, 4):
                                absolute(hg, 3 * st + lc // 3)
                    if st >= 1:
                        eng.wait_ge(sem(f"{p}_sb"), B * hg + st)
                        nc.scalar.activation(Sb[(st - 1) % 3][:, :, :], Sb[(st - 1) % 3][:, :, :], ACT.Exp).then_inc(sem(f"{p}_ex"), 1)
                    if ly == 1 and st < B:
                        absolute(hg, 3 * st + 2)
                    if ly == 0 and st == 2:
                        eng.dma_start(y_d[bass.ds((hg * FILL + E) * P, FILL * P), :].rearrange("(t p) d -> p t d", p=P),
                                      xnT[:, :, :].rearrange("p c t -> p (c t)")[:, 0:D].unsqueeze(1).to_broadcast([P, FILL, D])).then_inc(sem("m_fill"), 16)
                for n in range(2 * HA):
                    half, a = n // HA, n % HA
                    copy(ctxl[:, a, half * HALF:(half + 1) * HALF], PS[:, 3 + n % 2, 0:HALF], "lt", 8 * hg + n + 1, "lte")

            if ly == 0:
                body(0, first=True)
            with eng.Fori(g0 + (ly == 0), g0 + HG) as hg:
                body(hg)

        def att_vector(dve, ly):
            p, g0 = "a", ly * HG

            def rotate(hg, a, s):
                c, k = s // 2, 6 * a + s
                dve.wait_ge(sem(f"{p}_qb"), 24 * hg + k + 1)
                if k >= 2:
                    dve.wait_ge(sem(f"{p}_rope"), 24 * hg + k - 1)
                src = PS[:, 2 + 2 * (k % 2):4 + 2 * (k % 2), 0:HALF].rearrange("p i (b s) -> p i b s", b=BH)
                for j in range(2):
                    tab = ropeq[:, j, :, c, :].unsqueeze(2).to_broadcast([P, 2, BH, S])
                    ins = nc.vector.tensor_tensor(rt[k % 2][j][:, :, :].rearrange("p i (b s) -> p i b s", b=BH), src, tab, ALU.mult)
                ins.then_inc(sem(f"{p}_rt"), 1)

            def body(hg, first=False):
                if ly == 0:
                    for a in range(HA):
                        for s in range(6):
                            rotate(hg, a, s)
                            if first:
                                prep_vector(dve, 6 * a + s)
                    if first:
                        prep_add(dve, NQ - 1)
                for st in range(B + 2):
                    if 1 <= st <= B:
                        dve.wait_ge(sem(f"{p}_mt"), B * hg + st)
                        nc.vector.tensor_reduce(nmx[0:S, :], PS[0:S, 3, :].rearrange("p (a l) -> p a l", a=HA), AX, ALU.max,
                                                negate=True).then_inc(sem(f"{p}_nm"), 1)
                        dve.wait_ge(sem(f"{p}_nm"), B * hg + st)
                        nc.vector.tensor_tensor(diag[0:S, :, :], ident[0:S, 0:S].unsqueeze(1).to_broadcast([S, HA, S]),
                                                nmx[0:S, :].unsqueeze(2).to_broadcast([S, HA, S]), ALU.mult).then_inc(sem(f"{p}_dg"), 1)
                        dve.wait_ge(sem(f"{p}_mb"), B * hg + st)
                        sb = Sb[(st - 1) % 3][:, :, :]
                        nc.vector.tensor_tensor(sb, sb, PS[:, 4, 0:GW].unsqueeze(1).to_broadcast([P, LC, GW]),
                                                ALU.add).then_inc(sem(f"{p}_sb"), 1)
                    if st < B:
                        dve.wait_ge(sem(f"{p}_se"), LC * B * hg + LC * (st + 1))
                        nc.vector.tensor_reduce(mx[:, :], Sb[st % 3][:, :, :].rearrange("p c n -> p n c"), AX,
                                                ALU.max).then_inc(sem(f"{p}_mx"), 1)
                    if st >= 2:
                        dve.wait_ge(sem(f"{p}_z"), B * hg + st - 1)
                        if st >= 3:
                            dve.wait_ge(sem(f"{p}_cxe"), B * hg + st - 2)
                        nc.vector.reciprocal(rz[:, :], PS[:, 5, 0:GW]).then_inc(sem(f"{p}_rz"), 1)
                    if 1 <= st <= B:
                        dve.wait_ge(sem(f"{p}_ex"), B * hg + st)
                        nc.vector.tensor_reduce(sums[:, :], Sb[(st - 1) % 3][:, :, :].rearrange("p c n -> p n c"), AX,
                                                ALU.add).then_inc(sem(f"{p}_sum"), 1)
                    if st >= 2:
                        b = st - 2
                        dve.wait_ge(sem(f"{p}_rz"), B * hg + b + 1)
                        dve.wait_ge(sem(f"{p}_cx"), 2 * (B * hg + b + 1))
                        nc.vector.tensor_tensor(qc[:, :, b, :], PS[:, 6:8, 0:GW], rz[:, :].unsqueeze(1).to_broadcast([P, CC, GW]),
                                                ALU.mult).then_inc(sem(f"{p}_cxe"), 1)
                if ly == 1:
                    dve.wait_ge(sem("ab_done"), 24 * (hg - g0 + 1))
                    dve.wait_ge(sem("ab_sum"), hg - g0 + 1)
                    nc.vector.tensor_tensor(absum[:, :], absum[:, :], abpart[:, :], ALU.add).then_inc(sem("ab_sum"), 1)
                if not first:
                    dve.wait_ge(sem(f"{p}_stat"), NSTAT * hg + 2 * ly)
                if first or ly == 1:
                    dve.wait_ge(sem("a_tail"), ly + 1)
                for n in range(2 * MT):
                    m, nh, half = n // 2, n % 2, slice(n % 2 * 512, n % 2 * 512 + 512)
                    dve.wait_ge(sem(f"{p}_op"), 2 * MT * hg + n + 1)
                    to = X[:, m, half] if m < MT - 1 else tail[:, half]
                    nc.vector.tensor_tensor(to, PS[:, 2 + n % 4, :], to, ALU.add).then_inc(sem(f"{p}_add"), 1)
                    if 1 <= n <= NSTAT:
                        dve.wait_ge(sem(f"{p}_add"), 2 * MT * hg + n)
                        statistics((n - 1) // 2, (n - 1) % 2, f"{p}_stat")

            if ly == 1:
                nc.vector.memset(absum[:, :], 0.0).then_inc(sem("ab_sum"), 1)
            if ly == 0:
                body(0, first=True)
            with dve.Fori(g0 + (ly == 0), g0 + HG) as hg:
                body(hg)
            for nh in range(2):
                dve.wait_ge(sem("a_fold"), 2 * ly + nh + 1)
                xs = X[0:TW[-1], MT - 1, nh * 512:(nh + 1) * 512]
                nc.vector.tensor_tensor(xs, PS[0:TW[-1], 2 + nh, :], xs, ALU.add).then_inc(sem("a_folded"), 1)
            for nh in range(2):
                dve.wait_ge(sem("a_folded"), 2 * ly + nh + 1)
                statistics(MT - 1, nh, f"{p}_stat")

        def att_pool(pool, ly):
            p, g0 = "a", ly * HG

            def rope(hg, first=False):
                for k in range(NQ):
                    if first:
                        prep_pool(pool, k)
                    pool.wait_ge(sem(f"{p}_rt"), 24 * hg + k + 1)
                    if k >= 4:
                        pool.wait_ge(sem(f"{p}_qrm"), 12 * hg + (k - 4) // 2 + 1)
                    for i in range(2):
                        ins = nc.gpsimd.tensor_tensor(qrope[k % 4][:, i, :], rt[k % 2][0][:, i, :], rt[k % 2][1][:, 1 - i, :], ALU.add)
                    ins.then_inc(sem(f"{p}_rope"), 1)

            def absolute(hg, first):
                for st in range(8):
                    for w in range(3):
                        k = 3 * st + w
                        if not (first and k < 2):
                            pool.wait_ge(sem("ab_done"), 24 * hg + k - 1)
                        src = A["F"][8 * hg + st]
                        pool.dma_start(absin[k % 2][:, :], src[:, w * D:(w + 1) * D]).then_inc(sem(f"ab_in{k % 2}"), 16)

            if ly == 0:
                rope(0, first=True)
                pool.wait_ge(sem("ln_ev"), ln_count("a0", "ev", 2 * MT))
                nc.gpsimd.memset(tail[:, :], 0.0).then_inc(sem("a_tail"), 1)
                with pool.Fori(1, HG) as hg:
                    rope(hg)
            else:
                pool.wait_ge(sem("ln_ev"), ln_count("a1", "ev", 2 * MT))
                nc.gpsimd.memset(tail[:, :], 0.0).then_inc(sem("a_tail"), 1)
                absolute(0, True)
                with pool.Fori(1, HG) as hg:
                    absolute(hg, False)

        dvc = [0]

        def link(dve, ins):
            dvc[0] += 1
            ins.then_inc(sem("moe_dv"), 1)
            dve.wait_ge(sem("moe_dv"), dvc[0])

        def route_vector(dve):
            vt, tt, ts, stt = nc.vector, nc.vector.tensor_tensor, nc.vector.tensor_scalar, nc.vector.scalar_tensor_tensor

            def wide(a):
                return a.unsqueeze(2).to_broadcast([P, MT, E])

            def rows(a):
                return a.unsqueeze(1).to_broadcast([P, MT, E])

            dve.wait_ge(sem("m_gw"), 48)
            dve.wait_ge(sem("m_lgt"), 1)
            parts = PS[:, 6:8, :].rearrange("p b n -> p (b n)")[:, 0:MT * P].rearrange("p (m g e) -> p m e g", m=MT, g=QG)
            link(dve, vt.tensor_reduce(lg[:, :, :], parts, AX, ALU.add))
            link(dve, tt(lg[:, :, :], lg[:, :, :], rows(gb[:, :]), ALU.add))
            for m in range(MT):
                ins = vt.max(v8[:, m, :], lg[:, m, :])
            link(dve, ins)
            top, fourth = v8[:, :, 0], v8[:, :, TOPK - 1]
            tt(ex[:, :, :], lg[:, :, :], wide(top), ALU.subtract).then_inc(sem("m_exin"), 1)
            tt(eq[:, :, :], lg[:, :, :], wide(fourth), ALU.is_equal)
            link(dve, tt(sel[:, :, :], lg[:, :, :], wide(fourth), ALU.is_gt))
            for m in range(MT):
                vt.tensor_tensor_scan(csc[:, m, :], ones[:, 0:E], eq[:, m, :], 0.0, ALU.mult, ALU.add)
            link(dve, vt.tensor_reduce(need[:, :], sel[:, :, :], AX, ALU.add))
            link(dve, ts(need[:, :], need[:, :], -1.0, float(TOPK), ALU.mult, ALU.add))
            link(dve, tt(csc[:, :, :], csc[:, :, :], wide(need[:, :]), ALU.is_le))
            link(dve, tt(csc[:, :, :], csc[:, :, :], eq[:, :, :], ALU.mult))
            link(dve, tt(sel[:, :, :], sel[:, :, :], csc[:, :, :], ALU.add))
            dve.wait_ge(sem("m_ex"), 1)
            link(dve, tt(Gt[:, :, :], ex[:, :, :], sel[:, :, :], ALU.mult))
            tt(sel[:, :, :], sel[:, :, :], wide(cst[:, C_VAL:C_VAL + MT]), ALU.mult).then_inc(sem("m_sel"), 1)
            link(dve, vt.tensor_reduce(ssum[:, :], Gt[:, :, :], AX, ALU.add))
            link(dve, vt.reciprocal(ssum[:, :], ssum[:, :]))
            link(dve, tt(ssum[:, :], ssum[:, :], cst[:, C_VAL:C_VAL + MT], ALU.mult))
            tt(Gt[:, :, :], Gt[:, :, :], wide(ssum[:, :]), ALU.mult).then_inc(sem("m_gate"), 1)
            for m in range(MT):
                ins = vt.tensor_tensor_scan(csc[:, m, :], ones[:, 0:E], sel[:, m, :], 0.0, ALU.mult, ALU.add)
            dve.wait_ge(sem("m_cnt"), 1)
            link(dve, vt.tensor_reduce(cnt[:, :], PS[:, 6, 0:MT * E].rearrange("p (m e) -> p e m", m=MT), AX, ALU.add))
            link(dve, ts(nt[:, :], cnt[:, :], float(P), 1.0, ALU.is_gt, ALU.add))
            for q in range(2, -(-T // P)):
                link(dve, stt(nt[:, :], cnt[:, :], float(P * q), nt[:, :], ALU.is_gt, ALU.add))
            for k in range(TOPK):
                stt(eqk[k][:, :, :], csc[:, :, :], float(k + 1), sel[:, :, :], ALU.is_equal, ALU.mult)
            link(dve, vt.tensor_tensor_scan(tend[:, :], ones[:, 0:E], nt[:, :], 0.0, ALU.mult, ALU.add))
            tt(tst[:, :], tend[:, :], nt[:, :], ALU.subtract)
            link(dve, ts(cnt[:, :], tend[:, :], cst[:, C_PIX:C_PIX + 1], None, ALU.is_le))
            ts(tst[:, :], tst[:, :], float(P), None, ALU.mult)
            link(dve, vt.tensor_reduce(te_c[:, :], cnt[:, :], AX, ALU.add))
            dve.sem_inc(sem("m_te"), 1)
            dve.wait_ge(sem("m_rank"), 1)
            link(dve, tt(pos[:, :, :], PS[:, 5, 0:MT * E].rearrange("p (m e) -> p m e", m=MT), rows(tst[:, :]), ALU.add))
            for k in range(TOPK):
                ins = tt(eqk[k][:, :, :], eqk[k][:, :, :], pos[:, :, :], ALU.mult)
            link(dve, ins)
            for k in range(TOPK):
                ins = vt.tensor_reduce(slot[:, k, :], eqk[k][:, :, :], AX, ALU.add)
            link(dve, ins)
            sl = slot[:, :, :].rearrange("p k m -> p (k m)")
            link(dve, vt.tensor_copy(slot_i[:, :], sl))
            link(dve, ts(srow_i[:, :], slot_i[:, :], P - 1, None, ALU.bitwise_and))
            link(dve, vt.tensor_copy(srow[:, :], srow_i[:, :]))
            dve.sem_inc(sem("m_srow"), 1)
            link(dve, tt(sbase[:, :], sl, srow[:, :], ALU.subtract))
            vt.memset(idx[:, :], 0)
            for n in range(NK):
                k, m = n // MT, n % MT
                if n >= 4:
                    dve.wait_ge(sem("m_list"), n - 3)
                ts(oh_j[:, n % 4, :], cst[:, C_TILE:C_TILE + MAX_TILES], sbase[:, n:n + 1], cst[:, C_TID + m:C_TID + m + 1],
                   ALU.is_equal, ALU.mult).then_inc(sem("m_oh"), 1)
            dve.wait_ge(sem("m_list"), NK)
            vt.tensor_copy(idx[:, 0:MAX_TILES], PS[:, 7, 0:MAX_TILES]).then_inc(sem("m_idx"), 1)
            dve.wait_ge(sem("m_tet"), 1)
            ts(tst[0:1, :], tend[0:1, :], 2.0, None, ALU.mult)
            vt.tensor_copy(te_end[0:1, :], tend[0:1, :])
            link(dve, ts(te_f[0:1, :], PS[0:1, 1, 0:IDXW], float(E - 1), None, ALU.min))
            vt.tensor_copy(te2_i[0:1, :], tst[0:1, :])
            link(dve, vt.tensor_copy(te_i[0:1, :], te_f[0:1, :]))
            ts(tp_i[0:1, :], te_i[0:1, :], 1, None, ALU.bitwise_and)
            link(dve, ts(tst[0:1, 0:1], tend[0:1, E - 1:E], 1.0, None, ALU.add))
            link(dve, vt.tensor_copy(np_i[0:1, 0:1], tst[0:1, 0:1]))
            link(dve, ts(np_i[0:1, 1:2], np_i[0:1, 0:1], 1, None, ALU.arith_shift_right))
            ts(np_i[0:1, 2:3], np_i[0:1, 1:2], 1.0, None, ALU.subtract).then_inc(sem("m_tab"), 1)
            link(dve, ts(cnt[0:1, :], tend[0:1, :], 1.0, None, ALU.add))
            link(dve, vt.tensor_copy(te_odd[0][0:1, :], cnt[0:1, :]))
            ts(te_odd[0][0:1, :], te_odd[0][0:1, :], 1, None, ALU.arith_shift_right)
            ts(te_odd[1][0:1, :], te_end[0:1, :], 1, None, ALU.arith_shift_right)
            for n in range(2 * MT):
                m, nh = n // 2, n % 2
                dve.wait_ge(sem("m_bd"), n + 1)
                xs = X[:, m, nh * 512:(nh + 1) * 512]
                nc.vector.tensor_tensor(xs, PS[:, 4 + n % 2, :], xs, ALU.add).then_inc(sem("m_bda"), 1)
            for k in range(TOPK):
                ins = stt(eqk[k][:, :, :], csc[:, :, :], float(k + 1), sel[:, :, :], ALU.is_equal, ALU.mult)
            link(dve, ins)
            for k in range(TOPK):
                ins = tt(eqk[k][:, :, :], eqk[k][:, :, :], Gt[:, :, :], ALU.mult)
            link(dve, ins)
            for k in range(TOPK):
                vt.tensor_reduce(Gk[:, k, :], eqk[k][:, :, :], AX, ALU.add).then_inc(sem("m_gk"), 1)

        def logits(pe, m):
            if m not in (3, MT - 1):
                return
            h, tok = m // 4, slice(4 * P * (m // 4), (m + 1) * P)
            pe.wait_ge(sem("ln_ev"), ln_count("moe", "ev", 2 * m + 2))
            pe.wait_ge(sem("m_gw"), 48)
            for c in range(KC):
                g = c % QG
                mm = nc.tensor.matmul(PS[g * E:(g + 1) * E, 4 + h, 0:tok.stop - tok.start], gwT[:, c, :], hTm[:, c, tok],
                                      start=c < QG, stop=c >= KC - QG)
            mm.then_inc(sem("m_lg"), 1)

        def route_tensor(pe):
            pe.wait_ge(sem("m_lgc"), 2)
            for m in range(MT):
                mm = nc.tensor.transpose(PS[:, 6 + m // 4, (m % 4) * P:(m % 4 + 1) * P], lgT[:, m * P:(m + 1) * P], ident)
            mm.then_inc(sem("m_lgt"), 1)
            pe.wait_ge(sem("m_sel"), 1)
            tiles_of = lambda a, b: sel[:, a:b, :].rearrange("p m e -> p (m e)")
            nc.tensor.matmul(PS[:, 6, 0:MT * E], ones, tiles_of(0, MT), start=True, stop=True).then_inc(sem("m_cnt"), 1)
            nc.tensor.matmul(PS[:, 5, 0:MT * E], tri, tiles_of(0, MT), start=True, stop=False)
            for q in range(1, MT):
                mm = nc.tensor.matmul(PS[:, 5, q * E:MT * E], ones, tiles_of(0, MT - q), start=False, stop=q == MT - 1)
            mm.then_inc(sem("m_rank"), 1)
            pe.wait_ge(sem("m_te"), 1)
            nc.tensor.matmul(PS[0:1, 1, 0:P], te_c[:, :], ident, start=True, stop=True).then_inc(sem("m_tet"), 1)
            pe.wait_ge(sem("m_gate"), 1)
            for m in range(MT):
                bank = 2 + m // 4
                mm = nc.tensor.transpose(PS[0:E, bank, (m % 4) * P:(m % 4 + 1) * P], Gt[:, m, :], ident)
            mm.then_inc(sem("m_gt"), 1)
            for n in range(NK):
                pe.wait_ge(sem("m_ohs"), n + 1)
                pe.wait_ge(sem("m_oh"), n + 1)
                nc.tensor.matmul(PS[:, 7, 0:MAX_TILES], oh_s[:, n, :], oh_j[:, n % 4, :],
                                 start=n == 0, stop=n == NK - 1).then_inc(sem("m_list"), 1)

        def route_scalar(eng):
            for h in range(2):
                w = min(4 * P, TPAD - 4 * P * h)
                eng.wait_ge(sem("m_lg"), h + 1)
                nc.scalar.activation(lgT[:, 4 * P * h:4 * P * h + w], PS[:, 4 + h, 0:w], ACT.Copy).then_inc(sem("m_lgc"), 1)
            eng.wait_ge(sem("m_exin"), 1)
            nc.scalar.activation(ex[:, :, :], ex[:, :, :], ACT.Exp).then_inc(sem("m_ex"), 1)

        def moe_sync(sp):
            sp.wait_ge(sem("a_qc"), 16 * HG)
            sp.wait_ge(sem("m_fill"), 16 * HG)
            sp.dma_start(W2[:, 0, 0:W2_D], A["W2"][0, :, 0:W2_D]).then_inc(sem("m_wg0"), 16)
            sp.dma_start(W2[:, 0, W2_D:W2_N], A["W2"][0, :, W2_D:W2_N]).then_inc(sem("m_wd0"), 16)
            sp.wait_ge(sem("a_folded"), 2)
            sp.dma_start(gwT[:, :, :], A["gwT"].rearrange("p (c e) -> p c e", c=KC)).then_inc(sem("m_gw"), 16)
            sp.dma_start(gb[:, :], A["gb"].to_broadcast([P, E])).then_inc(sem("m_gw"), 16)
            sp.dma_start(bd, A["bd"]).then_inc(sem("m_gw"), 16)
            sp.dma_start(bias2[:, 0, :], A["b2"][0].to_broadcast([P, 2 * FI])).then_inc(sem("m_wg0"), 16)

            def first_half(e, q):
                sp.dma_start(W2[:, q, 0:W2_D], A["W2"][e, :, 0:W2_D]).then_inc(sem(f"m_wg{q}"), 16)
                sp.dma_start(bias2[:, q, :], A["b2"][e].to_broadcast([P, 2 * FI])).then_inc(sem(f"m_wg{q}"), 16)

            def second_half(e, q):
                sp.dma_start(W2[:, q, W2_D:W2_N], A["W2"][e, :, W2_D:W2_N]).then_inc(sem(f"m_wd{q}"), 16)

            def first_here(e, q):
                sp.wait_ge(sem(f"m_wg{q}"), 16 * (e - q) + 32)
                sp.sem_inc(sem("m_rg"), 1)

            def second_here(e, q):
                sp.wait_ge(sem(f"m_wd{q}"), 8 * (e - q) + 16)
                sp.sem_inc(sem("m_rd"), 1)

            def expert(e, q, first=False):
                done = sp.value_load(te_end[0:1, bass.ds(e - 2, 1)], min_val=1, max_val=MAX_TILES)
                sp.wait_ge(sem("m_act"), done)
                first_half(e, q)
                if not first:
                    done = sp.value_load(te2_i[0:1, bass.ds(e - 3, 1)], min_val=2, max_val=2 * MAX_TILES)
                    sp.wait_ge(sem("m_y"), done)
                second_half(e - 1, 1 - q)
                first_here(e, q)
                second_here(e - 1, 1 - q)

            for m in range(MT):
                sp.wait_ge(sem("ln_hn"), ln_count("moe", "hn", m + 1))
                sp.dma_start(h_d[m * P:(m + 1) * P, :], HN["moe"][m % 2][:, :]).then_inc(sem(f"moe_st{m % 2}"), 16)
            first_half(1, 1)
            for q in range(2):
                first_here(q, q)
            second_here(0, 0)
            sp.wait_ge(sem("m_tab"), 1)
            expert(2, 0, first=True)
            with sp.Fori(1, E // 2 - 1) as i:
                expert(2 * i + 1, 1)
                expert(2 * i + 2, 0)
            expert(E - 1, 1)
            done = sp.value_load(te2_i[0:1, E - 3:E - 2], min_val=2, max_val=2 * MAX_TILES)
            sp.wait_ge(sem("m_y"), done)
            second_half(E - 1, 1)
            second_here(E - 1, 1)

        def tiles(eng, first, step):
            first()
            eng.wait_ge(sem("m_tab"), 1)
            pairs = eng.value_load(np_i[0:1, 1:2], min_val=E // 2, max_val=MAX_PAIRS)
            for s in range(2):
                step(s, s)
            with eng.Fori(0, (MAX_PAIRS - 1) // RUN) as r:
                with eng.If(r * RUN + 1 < pairs):
                    with eng.Fori(0, RUN) as i:
                        with eng.If(r * RUN + i + 1 < pairs):
                            for s in range(2):
                                step(2 * RUN * r + 2 * i + 2 + s, s)
            before_last = eng.value_load(np_i[0:1, 2:3], min_val=E // 2 - 1, max_val=MAX_PAIRS - 1)
            return before_last

        def room(n):
            return n % 4 if n < 8 else (n - 4) % 6

        def use(n):
            return sum(room(i) == room(n) for i in range(n + 1))

        def signal(n):
            return f"m_yg{room(n)}" if room(n) < 4 else f"m_hs{room(n) - 4}"

        def before(n):
            return max([i for i in range(n) if room(i) == room(n)], default=None)

        def moe_pool(pool):
            def gather(j, q):
                if not (isinstance(j, int) and j < 2):
                    pool.wait_ge(sem("m_tp"), 2 * j - 2)
                nc.gpsimd.tensor_copy(idxc[q][:, :], idx[:, bass.ds(j, 1)]).then_inc(sem("m_ic"), 1)
                pool.wait_ge(sem("m_ic"), j + 1)
                pool.sem_inc(sem("m_go"), 1)
                nc.gpsimd.indirect_dma_start(out=hs[q][:, :], out_offset=None, in_=h_d[:, :],
                                             in_offset=bass.IndirectOffsetOnAxis(ap=idxc[q][:, :].bitcast(U32), axis=0)).then_inc(sem(f"m_hs{q}"), 16)

            def first():
                pool.wait_ge(sem("m_idx"), 1)
                pool.wait_ge(sem("moe_st0"), 16 * ((MT + 1) // 2))
                pool.wait_ge(sem("moe_st1"), 16 * (MT // 2))
                gather(0, 0)

            for n in range(NK):
                if n == 0:
                    pool.wait_ge(sem("m_srow"), 1)
                    pool.sem_inc(sem("m_go"), 1)
                nc.gpsimd.tensor_scalar(oh_s[:, n, :], cst[:, C_SLOT:C_SLOT + P], srow[:, n:n + 1], None,
                                        ALU.is_equal).then_inc(sem("m_ohs"), 1)
            last = tiles(pool, first, lambda j, s: gather(j + 1, 1 - s))
            pool.wait_ge(sem("m_gk"), TOPK)
            pool.wait_ge(sem("m_bda"), 2 * MT)
            pool.sem_inc(sem("m_go"), 1)

            def take(n):
                k, m = n // MT, n % MT
                if m == 0:
                    for q in range(2):
                        if k < TOPK - 1:
                            e = E - TOPK + k
                            stored = pool.value_load(te_odd[q][0:1, e:e + 1], min_val=(e + 1) // 2, max_val=MAX_PAIRS)
                            pool.wait_ge(sem(f"m_yo{q}"), 16 * stored)
                        else:
                            pool.wait_ge(sem(f"m_yo{q}"), 16 * last + 16)
                        pool.sem_inc(sem("m_go"), 1)
                if n == 8:
                    pool.wait_ge(sem("m_tp"), 4 * last + 6)
                    pool.sem_inc(sem("m_go"), 1)
                if before(n) is not None:
                    if before(n) < NPOOL:
                        pool.wait_ge(sem("m_padd"), before(n) + 1)
                    else:
                        pool.wait_ge(sem("m_yw"), before(n) + 1 - NPOOL)
                c = k * MT + m
                nc.gpsimd.indirect_dma_start(out=yg[room(n)][:, :], out_offset=None, in_=y_d[:, :],
                                             in_offset=bass.IndirectOffsetOnAxis(ap=slot_i[:, c:c + 1].bitcast(U32), axis=0)).then_inc(sem(signal(n)), 16)

            for n in range(4):
                take(n)
            for n in range(NK):
                k, m = n // MT, n % MT
                if n < NPOOL:
                    pool.wait_ge(sem(f"m_yg{room(n)}"), 16 * use(n))
                    nc.gpsimd.tensor_scalar(yg[room(n)][:, :], yg[room(n)][:, :], Gk[:, k, m:m + 1], None,
                                            ALU.mult).then_inc(sem("m_pw"), 1)
                    pool.wait_ge(sem("m_pw"), n + 1)
                    if k:
                        pool.wait_ge(sem("m_padd"), n - MT + 1)
                    nc.gpsimd.tensor_tensor(X[:, m, :], yg[room(n)][:, :], X[:, m, :], ALU.add).then_inc(sem("m_padd"), 1)
                if n + 4 < NK:
                    take(n + 4)

        def moe_tensor(pe):
            def turn(j, q, part):
                if part == 0:
                    pe.wait_ge(sem(f"m_hs{q}"), 8 * (j - q) + 16)
                if not (isinstance(j, int) and j == 0 and part == 0):
                    pe.wait_ge(sem("m_tpe"), 2 * j + part)
                for c in range(4):
                    cc = 4 * part + c
                    mm = nc.tensor.transpose(PS[:, 6, c * P:(c + 1) * P], hs[q][:, cc * P:(cc + 1) * P], ident)
                mm.then_inc(sem("m_tp"), 1)

            def gate_up(j, q, g, buf):
                bank = 2 + 2 * q + g
                for c in range(KC):
                    mm = nc.tensor.matmul(PS[:, bank, :], hT2[q][:, c, :],
                                          W2[:, bass.ds(buf, 1), c * 2 * FI + g * FI:c * 2 * FI + (g + 1) * FI].rearrange("p a n -> p (a n)"),
                                          start=c == 0, stop=c == KC - 1)
                mm.then_inc(sem("m_gu"), 1)

            def turn_act(j, q):
                pe.wait_ge(sem("m_act"), j + 1)
                for c in range(IC):
                    mm = nc.tensor.transpose(PS[:, 0, c * P:(c + 1) * P], act[q][:, c * P:(c + 1) * P], ident)
                mm.then_inc(sem("m_at"), 1)

            def down(j, q, buf, first=False):
                e = pe.value_load(te_i[0:1, bass.ds(j, 1)], min_val=0, max_val=E - 1)
                pe.wait_ge(sem("m_rd"), e + 1)
                pe.wait_ge(sem("m_ate"), j + 1)
                for nh in range(2):
                    if not first:
                        pe.wait_ge(sem("m_ye"), 2 * j - 1 + nh)
                    for c in range(IC):
                        o = W2_D + c * D + nh * 512
                        mm = nc.tensor.matmul(PS[:, 7 if nh == 0 else 1, :], actT[:, c, :],
                                              W2[:, bass.ds(buf, 1), o:o + 512].rearrange("p a n -> p (a n)"), start=c == 0, stop=c == IC - 1)
                    mm.then_inc(sem("m_y"), 1)

            def half(j):
                return pe.value_load(tp_i[0:1, bass.ds(j, 1)], min_val=0, max_val=1)

            def step(j, s):
                e = pe.value_load(te_i[0:1, bass.ds(j, 1)], min_val=0, max_val=E - 1)
                buf = half(j)
                turn(j + 1, 1 - s, 0)
                pe.wait_ge(sem("m_rg"), e + 1)
                pe.wait_ge(sem("m_tpe"), 2 * j + 2)
                gate_up(j, s, 0, buf)
                head = isinstance(j, int) and j == 0
                if not head:
                    turn_act(j - 1, 1 - s)
                turn(j + 1, 1 - s, 1)
                gate_up(j, s, 1, buf)
                if not head:
                    down(j - 1, 1 - s, half(j - 1), first=isinstance(j, int) and j == 1)

            def first():
                turn(0, 0, 0)
                turn(0, 0, 1)

            n = tiles(pe, first, step)
            turn_act(2 * n + 1, 1)
            down(2 * n + 1, 1, half(2 * n + 1))

        def moe_vector(dve):
            def step(j, s):
                buf = dve.value_load(tp_i[0:1, bass.ds(j, 1)], min_val=0, max_val=1)
                dve.wait_ge(sem("m_gu"), 2 * j + 1)
                nc.vector.tensor_tensor(gl[:, :], PS[:, 2 + 2 * s, :], bias2[:, bass.ds(buf, 1), 0:FI].rearrange("p a n -> p (a n)"),
                                        ALU.add).then_inc(sem("m_gl"), 1)
                dve.wait_ge(sem("m_gl"), 5 * j + 1)
                nc.vector.tensor_scalar(gl[:, :], gl[:, :], LIMIT, None, ALU.min).then_inc(sem("m_gl"), 1)
                dve.wait_ge(sem("m_gu"), 2 * j + 2)
                nc.vector.tensor_tensor(up1[:, :], PS[:, 3 + 2 * s, :], bias2[:, bass.ds(buf, 1), FI:2 * FI].rearrange("p a n -> p (a n)"),
                                        ALU.add).then_inc(sem("m_gl"), 1)
                dve.wait_ge(sem("m_gl"), 5 * j + 3)
                nc.vector.tensor_scalar(up1[:, :], up1[:, :], LIMIT, -LIMIT, ALU.min, ALU.max).then_inc(sem("m_gl"), 1)
                dve.wait_ge(sem("m_gl"), 5 * j + 4)
                nc.vector.scalar_tensor_tensor(up1[:, :], up1[:, :], 1.0, gl[:, :], ALU.add, ALU.mult).then_inc(sem("m_gl"), 1)
                dve.wait_ge(sem("m_gl"), 5 * j + 5)
                dve.wait_ge(sem("m_sg"), j + 1)
                nc.vector.tensor_tensor(act[s][:, :], up1[:, :], sg[:, :], ALU.mult).then_inc(sem("m_act"), 1)

            tiles(dve, lambda: None, step)
            for n in range(NK - NPOOL):
                k, m = KPOOL + n // MT, n % MT
                if k == KPOOL:
                    dve.wait_ge(sem("m_padd"), NPOOL - MT + m + 1)
                else:
                    dve.wait_ge(sem("m_add"), n - MT + 1)
                dve.wait_ge(sem("m_yw"), n + 1)
                nc.vector.tensor_tensor(X[:, m, :], PS[:, 2 * (n % 2) + 2:2 * (n % 2) + 4, :].rearrange("p h d -> p (h d)"), X[:, m, :],
                                        ALU.add).then_inc(sem("m_add"), 1)
                if k == TOPK - 1 and m >= 1:
                    dve.wait_ge(sem("m_add"), n)
                    for j in range(2):
                        statistics(m - 1, j, "m_stat")
            dve.wait_ge(sem("m_add"), NK - NPOOL)
            for j in range(2):
                statistics(MT - 1, j, "m_stat")

        def bias_tensor(pe):
            pe.wait_ge(sem("m_gte"), 2)
            for n in range(2 * MT):
                m, nh = n // 2, n % 2
                if n >= 2:
                    pe.wait_ge(sem("m_bda"), n - 1)
                nc.tensor.matmul(PS[:, 4 + n % 2, :], GT[:, m * P:(m + 1) * P], bd[:, nh * 512:(nh + 1) * 512],
                                 start=True, stop=True).then_inc(sem("m_bd"), 1)
            pe.wait_ge(sem("m_bda"), 2 * MT)

        def bias_scalar(eng):
            eng.wait_ge(sem("m_gt"), 1)
            nc.scalar.activation(GT[:, 0:512], PS[0:E, 2, :], ACT.Copy).then_inc(sem("m_gte"), 1)
            nc.scalar.activation(GT[:, 512:TPAD], PS[0:E, 3, 0:TPAD - 512], ACT.Copy).then_inc(sem("m_gte"), 1)

        def weigh_scalar(eng, ns, last):
            for n in ns:
                k, m, g = KPOOL + n // MT, n % MT, NPOOL + n
                eng.wait_ge(sem(signal(g)), 16 * use(g) + (16 * (last + 6 - room(g)) if room(g) >= 4 else 0))
                if n >= 2:
                    eng.wait_ge(sem("m_add"), n - 1)
                nc.scalar.activation(PS[:, 2 * (n % 2) + 2:2 * (n % 2) + 4, :].rearrange("p h d -> p (h d)"), yg[room(g)][:, :], ACT.Copy,
                                     scale=Gk[:, k, m:m + 1]).then_inc(sem("m_yw"), 1)

        def moe_scalar(eng):
            def turned(j, q, part):
                eng.wait_ge(sem("m_tp"), 2 * j + part + 1)
                nc.scalar.activation(hT2[q][:, 4 * part:4 * part + 4, :].rearrange("p c t -> p (c t)"), PS[:, 6, :],
                                     ACT.Copy).then_inc(sem("m_tpe"), 1)

            def turned_act(j):
                eng.wait_ge(sem("m_at"), j + 1)
                nc.scalar.activation(actT[:, :, :].rearrange("p c t -> p (c t)"), PS[:, 0, :], ACT.Copy).then_inc(sem("m_ate"), 1)

            def store(j, q, first):
                if not first:
                    eng.wait_ge(sem(f"m_yo{q}"), 8 * (j - q))
                if first:
                    eng.wait_ge(sem("m_fill"), 16 * HG)
                for nh in range(2):
                    eng.wait_ge(sem("m_y"), 2 * j + nh + 1)
                    nc.scalar.activation(ysb[q][:, nh * 512:(nh + 1) * 512], PS[:, 7 if nh == 0 else 1, :],
                                         ACT.Copy).then_inc(sem("m_ye"), 1)
                eng.wait_ge(sem("m_ye"), 2 * j + 2)
                eng.dma_start(y_d[bass.ds(j * P, P), :], ysb[q][:, :]).then_inc(sem(f"m_yo{q}"), 16)

            def step(j, s):
                head = isinstance(j, int) and j == 0
                turned(j + 1, 1 - s, 0)
                if not head:
                    turned_act(j - 1)
                turned(j + 1, 1 - s, 1)
                eng.wait_ge(sem("m_gl"), 5 * j + 2)
                nc.scalar.activation(sg[:, :], gl[:, :], ACT.Sigmoid, scale=ALPHA).then_inc(sem("m_sg"), 1)
                if not head:
                    store(j - 1, 1 - s, isinstance(j, int) and j <= 2)

            def first():
                turned(0, 0, 0)
                turned(0, 0, 1)

            n = tiles(eng, first, step)
            turned_act(2 * n + 1)
            eng.wait_ge(sem("m_gk"), TOPK)
            eng.wait_ge(sem("m_act"), 2 * n + 2)
            weigh_scalar(eng, range(EARLY), n)
            store(2 * n + 1, 1, False)
            weigh_scalar(eng, range(EARLY, NK - NPOOL), n)

        def down_steps(blk):
            steps = [("last", MT - 1, nh) for nh in range(2)] + [("tile", n // 2, n % 2) for n in range(2 * MT - 2)]
            if blk == NBLK - 1:
                steps[8:8] = [("sum", MT - 1, nh) for nh in range(2)]
            return steps

        def ffn_sync(sp):
            sp.wait_ge(sem("a_folded"), 4)
            sp.wait_ge(sem("ab_done"), 24 * HG)

            def load(g, q):
                sp.dma_start(stg[q][:, :, :], A["F"][g].rearrange("p (w n) -> p w n", w=3)).then_inc(sem(f"f_in{q}"), 16)

            for q in range(2):
                load(q, q)
            with sp.Fori(1, EC // 2) as i:
                for q in range(2):
                    sp.wait_ge(sem("f_qd"), 2 * i + q - 1)
                    load(2 * i + q, q)
            for m in range(MT):
                at = down_steps(NBLK - 1).index(("sum" if m == MT - 1 else "tile", m, 1))
                sp.wait_ge(sem("f_add"), 2 * MT * (NBLK - 1) + at + 1)
                sp.dma_start(out_t[m * P:m * P + TW[m], :], X[0:TW[m], m, :]).then_inc(sem("out"), 16)
            sp.wait_ge(sem("out"), 16 * MT)

        def ffn_scales(dve):
            sc = [0]

            def then(ins):
                sc[0] += 1
                ins.then_inc(sem("f_sc"), 1)
                dve.wait_ge(sem("f_sc"), sc[0])

            dve.wait_ge(sem("ab_sum"), HG + 1)
            nc.vector.tensor_reduce(tsum[:, :], absum[:, :].rearrange("p (s w) -> p w s", w=3), AX, ALU.add).then_inc(sem("f_ts"), 1)
            dve.wait_ge(sem("f_tot"), 1)
            then(nc.vector.tensor_scalar(tern[:, :], PS[:, 7, 0:3], 1.0 / (FE * D), TERN_EPS, ALU.mult, ALU.add))
            nc.vector.tensor_scalar(thr[:, :], tern[:, :], 0.5, None, ALU.mult).then_inc(sem("f_thr"), 1)
            nc.vector.tensor_scalar(nthr[:, :], tern[:, :], -0.5, None, ALU.mult)
            nc.vector.tensor_scalar(upsc[:, :], tern[:, 0:1], -1.0 / XS, None, ALU.mult)
            then(nc.vector.tensor_tensor(cd1[:, :], tern[:, 0:1], tern[:, 1:2], ALU.mult))
            then(nc.vector.tensor_tensor(cd2[:, :], cd1[:, :], tern[:, 2:3], ALU.mult))
            then(nc.vector.tensor_scalar(cd1[:, :], cd2[:, :], -1.0 / HSC, None, ALU.mult))

        def ffn_vector(dve):
            def low(m):
                w = TW[m]
                for h in range(2):
                    dve.wait_ge(sem("ffn_hi"), 2 * m + h + 1)
                    src = PS[:, 2 * (m % 2) + h, :].rearrange("p (c t) -> p c t", c=4)[:, :, 0:w]
                    cols = slice(m * P, m * P + w)
                    nc.vector.scalar_tensor_tensor(xh[1][:, 4 * h:4 * h + 4, cols], src, XS, xh[0][:, 4 * h:4 * h + 4, cols],
                                                   ALU.mult, ALU.subtract).then_inc(sem("ln_ev"), 1)

            ffn_scales(dve)
            for m in range(MT):
                ln_tile(dve, "ffn", m)
                if m >= 1:
                    low(m - 1)
            low(MT - 1)

            def ternary(dst, q, w, done):
                nc.vector.scalar_tensor_tensor(dst, stg[q][:, w, :], nthr[:, w:w + 1], gtq[q][:, w, :],
                                               ALU.is_lt, ALU.subtract).then_inc(sem(done), 1)

            def quantise_up_gate(blk, e, q):
                g = blk * EB + e
                dve.wait_ge(sem("f_gt"), 3 * g + 3)
                if not (isinstance(g, int) and g < 2):
                    dve.wait_ge(sem("f_ug"), 2 * g - 2)
                for w in range(2):
                    ternary(wq[q][:, w, :, :].rearrange("p c n -> p (c n)"), q, w, "f_q")

            def quantise_down(blk, e, q):
                if blk:
                    dve.wait_ge(sem("f_dn"), 2 * MT * blk)
                ternary(wdq[:, bass.ds(e, 1), :].rearrange("p a n -> p (a n)"), q, 2, "f_qd")

            def quantise(blk, e, q):
                quantise_up_gate(blk, e, q)
                quantise_down(blk, e, q)

            def hidden(blk, e, q):
                g = blk * EB + e
                dve.wait_ge(sem("f_sg"), g + 1)
                if not (isinstance(g, int) and g < 2):
                    dve.wait_ge(sem("f_lo"), g - 1)
                nc.vector.scalar_tensor_tensor(sgf[q][:, :, :], PS[:, 4 * q:4 * q + 2, 0:HALF], HSC / (XS * XS), sgf[q][:, :, :],
                                               ALU.mult, ALU.mult).then_inc(sem("f_hv"), 1)
                dve.wait_ge(sem("f_hv"), g + 1)
                dve.wait_ge(sem("f_ug"), 2 * g + 2)
                nc.vector.tensor_tensor(hid[q][:, :, :], PS[:, 4 * q + 2:4 * q + 4, 0:HALF], sgf[q][:, :, :],
                                        ALU.mult).then_inc(sem("f_hid"), 1)

            for blk in range(NBLK):
                if blk == 0:
                    quantise_up_gate(0, 0, 0)
                    quantise_up_gate(0, 1, 1)
                for q in range(2):
                    quantise_down(blk, q, q)
                hidden(blk, 0, 0)
                quantise(blk, 2, 0)
                hidden(blk, 1, 1)
                with dve.Fori(1, EB // 2 - 1) as i:
                    for q in range(2):
                        quantise(blk, 2 * i + q + 1, 1 - q)
                        hidden(blk, 2 * i + q, q)
                quantise(blk, EB - 1, 1)
                hidden(blk, EB - 2, 0)
                hidden(blk, EB - 1, 1)
                if blk < NBLK - 1:
                    quantise_up_gate(blk + 1, 0, 0)
                    quantise_up_gate(blk + 1, 1, 1)
                for n, (kind, m, nh) in enumerate(down_steps(blk)):
                    dve.wait_ge(sem("f_dn"), 2 * MT * blk + n + 1)
                    half = slice(nh * 512, (nh + 1) * 512)
                    if kind == "last" and nh == 0 and blk == 0:
                        dve.wait_ge(sem("f_tail"), 1)
                    if kind == "sum":
                        xs = X[0:TW[m], m, half]
                        nc.vector.tensor_tensor(xs, PS[0:TW[m], n % 8, :], xs, ALU.add).then_inc(sem("f_add"), 1)
                    else:
                        to = X[:, m, half] if kind == "tile" else tailf[:, half]
                        nc.vector.scalar_tensor_tensor(to, PS[:, n % 8, :], cd1[:, :], to, ALU.mult, ALU.add).then_inc(sem("f_add"), 1)

        def ffn_pool(pool):
            def greater(g, q):
                if not (isinstance(g, int) and g < 2):
                    pool.wait_ge(sem("f_qd"), g - 1)
                pool.wait_ge(sem(f"f_in{q}"), 8 * (g - q) + 16)
                pool.sem_inc(sem("f_go"), 1)
                for w in range(3):
                    nc.gpsimd.tensor_scalar(gtq[q][:, w, :], stg[q][:, w, :], thr[:, w:w + 1], None,
                                            ALU.is_gt).then_inc(sem("f_gt"), 1)

            def low(blk, e, q):
                g = blk * EB + e
                if blk:
                    pool.wait_ge(sem("f_dn"), 2 * MT * blk)
                pool.wait_ge(sem("f_hi"), g + 1)
                nc.gpsimd.tensor_tensor(hh[1][:, bass.ds(e, 1), :].rearrange("p a t -> p (a t)"), hid[q][:, :, :].rearrange("p h t -> p (h t)"),
                                        hh[0][:, bass.ds(e, 1), :].rearrange("p a t -> p (a t)"), ALU.subtract).then_inc(sem("f_lo"), 1)

            pool.wait_ge(sem("a_folded"), 4)
            nc.gpsimd.memset(tailf[:, :], 0.0).then_inc(sem("f_tail"), 1)
            pool.wait_ge(sem("f_thr"), 1)
            for q in range(2):
                greater(q, q)
            for blk in range(NBLK):
                with pool.Fori(0, EB // 2 - 1) as i:
                    for q in range(2):
                        greater(2 * i + q + 2 + blk * EB, q)
                        low(blk, 2 * i + q, q)
                for q in range(2):
                    if blk < NBLK - 1:
                        greater((blk + 1) * EB + q, q)
                    low(blk, EB - 2 + q, q)

        def ffn_scalar(eng):
            def chunk(blk, e, q):
                g = blk * EB + e
                eng.wait_ge(sem("f_ug"), 2 * g + 1)
                nc.scalar.activation(sgf[q][:, :, :], PS[:, 4 * q:4 * q + 2, 0:HALF], ACT.Sigmoid,
                                     scale=upsc[:, 0:1]).then_inc(sem("f_sg"), 1)
                eng.wait_ge(sem("f_hid"), g + 1)
                if blk:
                    eng.wait_ge(sem("f_dn"), 2 * MT * blk)
                nc.scalar.activation(hh[0][:, bass.ds(e, 1), :].rearrange("p a t -> p (a t)"), hid[q][:, :, :].rearrange("p h t -> p (h t)"),
                                     ACT.Copy).then_inc(sem("f_hi"), 1)

            eng.wait_ge(sem("f_sc"), 4)
            for blk in range(NBLK):
                with eng.Fori(0, EB // 2) as i:
                    for q in range(2):
                        chunk(blk, 2 * i + q, q)

        def ffn_tensor(pe):
            def up_gate(blk, e, q):
                g = blk * EB + e
                pe.wait_ge(sem("f_q"), 2 * g + 2)
                if not (isinstance(g, int) and g < 2):
                    pe.wait_ge(sem("f_hid"), g - 1)
                for w in range(2):
                    for c in range(KC):
                        for part in range(2):
                            for half in range(2):
                                mm = nc.tensor.matmul(PS[:, 4 * q + 2 * w + half, 0:HALF], wq[q][:, w, c, :],
                                                      xh[part][:, c, half * HALF:(half + 1) * HALF],
                                                      start=c == 0 and part == 0, stop=c == KC - 1 and part == 1)
                    mm.then_inc(sem("f_ug"), 1)

            pe.wait_ge(sem("ln_ev"), ln_count("ffn", "ev", 2 * MT))
            for blk in range(NBLK):
                if blk:
                    pe.wait_ge(sem("f_add"), 2 * MT * blk)
                for q in range(2):
                    up_gate(blk, q, q)
                with pe.Fori(1, EB // 2) as i:
                    for q in range(2):
                        up_gate(blk, 2 * i + q, q)
                pe.wait_ge(sem("f_hi"), EB * (blk + 1))
                pe.wait_ge(sem("f_lo"), EB * (blk + 1))
                pe.wait_ge(sem("f_qd"), EB * (blk + 1))
                for n, (kind, m, nh) in enumerate(down_steps(blk)):
                    if n >= 8:
                        pe.wait_ge(sem("f_add"), 2 * MT * blk + n - 7)
                    half = slice(nh * 512, (nh + 1) * 512)
                    if kind == "sum":
                        mm = nc.tensor.matmul(PS[0:TW[m], n % 8, :], cst[:, C_FOLD:C_FOLD + TW[m]], tailf[:, half], start=True, stop=True)
                    else:
                        for c in range(EB):
                            for part in range(2):
                                if kind == "tile":
                                    mm = nc.tensor.matmul(PS[:, n % 8, :], hh[part][:, c, m * P:(m + 1) * P], wdq[:, c, half],
                                                          start=c == 0 and part == 0, stop=c == EB - 1 and part == 1)
                                else:
                                    g = c % HA
                                    mm = nc.tensor.matmul(PS[g * TW[m]:(g + 1) * TW[m], n % 8, :], hh[part][:, c, m * P:T], wdq[:, c, half],
                                                          start=c < HA and part == 0, stop=c >= EB - HA and part == 1)
                    mm.then_inc(sem("f_dn"), 1)

        ORDER = [s for s in ("a0", "moe", "a1", "ffn") if s in stages]
        DONE = {"a0": ("a_folded", 2), "moe": ("m_add", NK - NPOOL), "a1": ("a_folded", 4)}

        STAT = {"a0": ("x_stat", 2 * MT), "moe": ("a_stat", NSTAT * HG + 2), "a1": ("m_stat", 2 * MT), "ffn": ("a_stat", 2 * NSTAT * HG + 4)}

        @block.sync
        def _(sp):
            prep_sync(sp)
            for p in ORDER:
                if p[0] == "a":
                    att_sync(sp, int(p[1]))
                elif p == "moe":
                    moe_sync(sp)
                else:
                    ffn_sync(sp)
            if "ffn" not in stages:
                s, v = DONE[ORDER[-1]]
                sp.wait_ge(sem(s), v)
                for m in range(MT):
                    sp.dma_start(out_t[m * P:m * P + TW[m], :], X[0:TW[m], m, :]).then_inc(sem("out"), 16)
                sp.wait_ge(sem("out"), 16 * MT)

        @block.vector
        def _(dve):
            for m in range(MT):
                dve.wait_ge(sem(f"x_in{m // 2}"), 16 * min(2, MT - m // 2 * 2))
                for j in range(2):
                    statistics(m, j, "x_stat")
            for p in ORDER:
                ln_vector(dve, p, STAT[p])
                if p != "ffn":
                    for m in range(MT):
                        ln_tile(dve, p, m, stored=p == "moe")
                if p == "a0":
                    dve.wait_ge(sem("rope_in"), 16)
                if p[0] == "a":
                    att_vector(dve, int(p[1]))
                elif p == "moe":
                    route_vector(dve)
                    moe_vector(dve)
                else:
                    ffn_vector(dve)

        @block.scalar
        def _(eng):
            for p in ORDER:
                ln_scalar(eng, p, {"moe": hTm, "ffn": xh}.get(p, xnT), pad=p == "moe")
                if p[0] == "a":
                    att_scalar(eng, int(p[1]))
                elif p == "moe":
                    route_scalar(eng)
                    bias_scalar(eng)
                    moe_scalar(eng)
                else:
                    ffn_scalar(eng)

        @block.gpsimd
        def _(pool):
            prep_zero(pool)
            for p in ORDER:
                if p[0] == "a":
                    att_pool(pool, int(p[1]))
                elif p == "moe":
                    moe_pool(pool)
                else:
                    ffn_pool(pool)

        @block.tensor
        def _(pe):
            pe.wait_ge(sem("cst_in"), 16)
            for p in ORDER:
                if p == "ffn":
                    pe.wait_ge(sem("f_ts"), 1)
                    nc.tensor.matmul(PS[:, 7, 0:3], ones, tsum[:, :], start=True, stop=True).then_inc(sem("f_tot"), 1)
                ln_tensor(pe, p, then=(lambda m: logits(pe, m)) if p == "moe" else None)
                if p[0] == "a":
                    pe.wait_ge(sem("ln_ev"), ln_count(p, "ev", 2 * MT))
                    att_tensor(pe, int(p[1]))
                elif p == "moe":
                    route_tensor(pe)
                    bias_tensor(pe)
                    moe_tensor(pe)
                else:
                    ffn_tensor(pe)


def layout(i):
    def c(a):
        return np.ascontiguousarray(a)

    arr = {"x": c(np.asarray(i["x"]).reshape(T, D)), "ctx": c(np.asarray(i["ctx_512"]))}
    for ly in range(2):
        g = {n: np.asarray(i[f"L{ly}_xattn_{n}"]) for n in ("Wq", "w_kc_q", "w_kc_kv", "W_qr", "W_kr", "Wo")}
        wc = np.zeros((H, P, WC_N), np.float32)
        wc[:, :, WC_R:WC_K] = g["W_qr"].reshape(H, QC, P, R).transpose(0, 2, 1, 3).reshape(H, P, QC * R)
        wkr = g["W_kr"].transpose(0, 2, 1)
        if ly == 0:
            arr["WQ0"] = c(g["Wq"].reshape(H, K, KC, P).transpose(0, 3, 2, 1).reshape(H, P, KC * K))
            wc[:, :, WC_C:WC_R] = g["w_kc_q"]
            wc[:, 0:R, WC_K:WC_K + DC] = wkr
            wc[:, R:2 * R, WC_K + DC:] = wkr
        else:
            arr["WQ1"] = c(g["Wq"].reshape(H, K, D))
            wc[:, :, WC_C:WC_R] = g["w_kc_q"].reshape(H, K, QC, P).transpose(0, 3, 2, 1).reshape(H, P, DQ)
            wc = c(wc[:, :, 0:WC_K])
            wk = np.zeros((HG, P, HA, DC), np.float32)
            for a in range(HA):
                wk[:, (a % 2) * R:(a % 2 + 1) * R, a] = wkr[a::HA]
            arr["WK"] = wk.reshape(HG, P, HA * DC)
        wb = np.zeros((HG, P, WB_N), np.float32)
        wb[:, :, WB_V:WB_O] = g["w_kc_kv"].reshape(HG, HA, K, CC, P).transpose(0, 4, 1, 3, 2).reshape(HG, P, HA * CC * K)
        wb[:, :, WB_O:] = g["Wo"].reshape(D, HG, HA, K).transpose(1, 3, 2, 0).reshape(HG, P, HA * D)
        arr[f"WC{ly}"], arr[f"WB{ly}"] = wc, wb
    f = {n: np.asarray(i[f"L0_ffn_{n}"]) for n in ("gate_w", "gate_b", "w_gate", "b_gate", "w_up", "b_up", "w_down", "b_down")}
    arr["gwT"] = c(f["gate_w"].reshape(E, KC, P).transpose(2, 1, 0).reshape(P, KC * E))
    arr["gb"] = c(f["gate_b"].reshape(1, E))
    arr["bd"] = c(f["b_down"])
    w2 = np.zeros((E, P, W2_N), np.float32)
    gu = w2[:, :, 0:W2_D].reshape(E, P, KC, 2, FI)
    gu[:, :, :, 0] = f["w_gate"].reshape(E, KC, P, FI).transpose(0, 2, 1, 3)
    gu[:, :, :, 1] = f["w_up"].reshape(E, KC, P, FI).transpose(0, 2, 1, 3)
    w2[:, :, 0:W2_D] = gu.reshape(E, P, W2_D)
    w2[:, :, W2_D:] = f["w_down"].reshape(E, IC, P, D).transpose(0, 2, 1, 3).reshape(E, P, IC * D)
    arr["W2"] = w2
    arr["b2"] = c(np.concatenate([f["b_gate"], f["b_up"]], 1).reshape(E, 1, 2 * FI))
    t = {n: np.asarray(i[f"L1_ffn_W_{n}"]) for n in ("up", "gate", "down")}
    fw = np.zeros((EC, P, 3, D), np.float32)
    for w, n in enumerate(("up", "gate")):
        fw[:, :, w] = t[n].reshape(EC, P, KC, P).transpose(0, 3, 2, 1).reshape(EC, P, D)
    fw[:, :, 2] = t["down"].reshape(D, EC, P).transpose(1, 2, 0)
    arr["F"] = fw.reshape(EC, P, 3 * D)
    arr.update(constants())
    return arr


def kernel(**inputs):
    from concourse import bacc
    from concourse.bass_utils import run_bass_kernel_spmd

    arrays = layout(inputs)
    nc = bacc.Bacc("TRN2", target_bir_lowering=False, num_devices=1)
    tensors = {n: nc.dram_tensor(f"in_{n}", list(a.shape), mybir.dt.from_np(a.dtype), kind="ExternalInput").ap() for n, a in arrays.items()}
    tensors["out"] = nc.dram_tensor("out", [T, D], F32, kind="ExternalOutput").ap()
    build(nc, tensors)
    r = run_bass_kernel_spmd(nc, [{f"in_{n}": a for n, a in arrays.items()}], core_ids=[0])
    return np.asarray(r.results[0]["out"]).reshape(B, S, D)
```
